# Optimizing a Trainium2 kernel written in Bass

```python
import numpy as np
import jax
import jax.numpy as jnp

def _softmax(x, axis=-1):
    return jax.nn.softmax(x, axis=axis)

def _gelu(x):
    return jax.nn.gelu(x, approximate=True)

def _silu(x):
    return jax.nn.silu(x)

def _sigmoid(x):
    return jax.nn.sigmoid(x)

def _layernorm(x, axis=-1, eps=1e-05):
    m = jnp.mean(x, axis=axis, keepdims=True)
    v = jnp.var(x, axis=axis, keepdims=True)
    return (x - m) / jnp.sqrt(v + eps)

def _scatter_add(tgt, idx, src, axis=0):
    return tgt.at[idx].add(src)

def _segment_sum(src, seg, n):
    return jax.ops.segment_sum(src, seg, n)
kernel_name = 'mk_prb_d1_jaxref_r8_62d4ed'

def setup_inputs(seed: int=0):
    np.random.seed(seed)
    _w = jnp.asarray

    def _L0_attn_setup():
        import jax, jax.numpy as jnp
        import numpy as np
        B, T, D = (1, 256, 128)
        H = 16
        HD = D // H
        WINDOW = 128
        NEG = -10000000000.0

        def _mask(t):
            i = jnp.arange(t)[:, None]
            j = jnp.arange(t)[None, :]
            return ((j <= i) & (j >= i - WINDOW)).astype(jnp.float32)

        def _genetic_fitness(g):
            t = g.shape[2]
            dot = jnp.einsum('bhid,bhjd->bhij', g, g)
            nrm = jnp.linalg.norm(g, axis=-1)
            corr = dot / (nrm[..., :, None] * nrm[..., None, :] + 1e-08)
            corr = jnp.nan_to_num(corr, nan=0.0, posinf=1.0, neginf=-1.0)
            m = _mask(t)[None, None]
            corr = corr * m
            corr = (corr + 1.0) / 2.0
            gene_means = jnp.mean(corr, axis=3)
            denom = gene_means + 0.5
            sum_inv = jnp.sum(1.0 / denom, axis=2, keepdims=True)
            gene_fitness = 1.0 / (denom * sum_inv)
            weighted = corr * gene_fitness[..., None]
            masked = weighted * m + (1.0 - m) * NEG
            return jax.nn.softmax(masked, axis=-1)
        key = jax.random.key(seed)
        ks = jax.random.split(key, 7)
        s = 1.0 / np.sqrt(D)
        return {'x': jax.random.normal(ks[0], (B, T, D), jnp.float32), 'Wg': jax.random.normal(ks[1], (D, D), jnp.float32) * s, 'bg': jax.random.normal(ks[2], (D,), jnp.float32) * 0.01, 'Wv': jax.random.normal(ks[3], (D, D), jnp.float32) * s, 'bv': jax.random.normal(ks[4], (D,), jnp.float32) * 0.01, 'Wo': jax.random.normal(ks[5], (D, D), jnp.float32) * s, 'bo': jax.random.normal(ks[6], (D,), jnp.float32) * 0.01}
    _L0_attn_in = _L0_attn_setup()

    def _L0_ffn_setup():
        import jax, jax.numpy as jnp
        import numpy as np
        TOP_K = 4
        CAP_FACTOR = 4

        def swiglu(x, w1, w2, w3):
            return jax.nn.silu(x @ w1) * (x @ w3) @ w2
        key = jax.random.key(seed)
        ks = jax.random.split(key, 8)
        B, S, D, H, E = (2, 256, 128, 64, 32)
        Hs = 2 * H
        sd = lambda *sh: 1.0 / np.sqrt(sh[-2])
        x = jax.random.normal(ks[0], (B, S, D), dtype=jnp.float32)
        Wg = jax.random.normal(ks[1], (D, E), dtype=jnp.float32) * (1.0 / np.sqrt(D))
        W1 = jax.random.normal(ks[2], (E, D, H), dtype=jnp.float32) * (1.0 / np.sqrt(D))
        W3 = jax.random.normal(ks[3], (E, D, H), dtype=jnp.float32) * (1.0 / np.sqrt(D))
        W2 = jax.random.normal(ks[4], (E, H, D), dtype=jnp.float32) * (1.0 / np.sqrt(H))
        Ws1 = jax.random.normal(ks[5], (D, Hs), dtype=jnp.float32) * (1.0 / np.sqrt(D))
        Ws3 = jax.random.normal(ks[6], (D, Hs), dtype=jnp.float32) * (1.0 / np.sqrt(D))
        Ws2 = jax.random.normal(ks[7], (Hs, D), dtype=jnp.float32) * (1.0 / np.sqrt(Hs))
        return {'x': x, 'Wg': Wg, 'W1': W1, 'W2': W2, 'W3': W3, 'Ws1': Ws1, 'Ws2': Ws2, 'Ws3': Ws3}
    _L0_ffn_in = _L0_ffn_setup()
    _d = {'L0_attn_x': _L0_attn_in['x'], 'L0_attn_Wg': _L0_attn_in['Wg'], 'L0_attn_bg': _L0_attn_in['bg'], 'L0_attn_Wv': _L0_attn_in['Wv'], 'L0_attn_bv': _L0_attn_in['bv'], 'L0_attn_Wo': _L0_attn_in['Wo'], 'L0_attn_bo': _L0_attn_in['bo'], 'L0_ffn_Wg': _L0_ffn_in['Wg'], 'L0_ffn_W1': _L0_ffn_in['W1'], 'L0_ffn_W2': _L0_ffn_in['W2'], 'L0_ffn_W3': _L0_ffn_in['W3'], 'L0_ffn_Ws1': _L0_ffn_in['Ws1'], 'L0_ffn_Ws2': _L0_ffn_in['Ws2'], 'L0_ffn_Ws3': _L0_ffn_in['Ws3']}
    _x0 = _d['L0_attn_x']
    _d['L0_attn_x'] = jax.random.normal(jax.random.fold_in(jax.random.key(seed), 1), (8, 256, 128), dtype=_x0.dtype)
    del _x0
    return _d

def reference(L0_attn_x, L0_attn_Wg, L0_attn_bg, L0_attn_Wv, L0_attn_bv, L0_attn_Wo, L0_attn_bo, L0_ffn_Wg, L0_ffn_W1, L0_ffn_W2, L0_ffn_W3, L0_ffn_Ws1, L0_ffn_Ws2, L0_ffn_Ws3):

    def _L0_attn_ref(x, Wg, bg, Wv, bv, Wo, bo):
        import jax, jax.numpy as jnp
        import numpy as np
        B, T, D = (1, 256, 128)
        H = 16
        HD = D // H
        WINDOW = 128
        NEG = -10000000000.0

        def _mask(t):
            i = jnp.arange(t)[:, None]
            j = jnp.arange(t)[None, :]
            return ((j <= i) & (j >= i - WINDOW)).astype(jnp.float32)

        def _genetic_fitness(g):
            t = g.shape[2]
            dot = jnp.einsum('bhid,bhjd->bhij', g, g)
            nrm = jnp.linalg.norm(g, axis=-1)
            corr = dot / (nrm[..., :, None] * nrm[..., None, :] + 1e-08)
            corr = jnp.nan_to_num(corr, nan=0.0, posinf=1.0, neginf=-1.0)
            m = _mask(t)[None, None]
            corr = corr * m
            corr = (corr + 1.0) / 2.0
            gene_means = jnp.mean(corr, axis=3)
            denom = gene_means + 0.5
            sum_inv = jnp.sum(1.0 / denom, axis=2, keepdims=True)
            gene_fitness = 1.0 / (denom * sum_inv)
            weighted = corr * gene_fitness[..., None]
            masked = weighted * m + (1.0 - m) * NEG
            return jax.nn.softmax(masked, axis=-1)
        b, t, d = x.shape
        g = x @ Wg.T + bg
        v = x @ Wv.T + bv
        g = g.reshape(b, t, H, HD).transpose(0, 2, 1, 3)
        v = v.reshape(b, t, H, HD).transpose(0, 2, 1, 3)
        attn = _genetic_fitness(g)
        out = jnp.einsum('bhij,bhjd->bhid', attn, v)
        out = out.transpose(0, 2, 1, 3).reshape(b, t, d)
        return out @ Wo.T + bo

    def _L0_ffn_ref(x, Wg, W1, W2, W3, Ws1, Ws2, Ws3):
        import jax, jax.numpy as jnp
        import numpy as np
        TOP_K = 4
        CAP_FACTOR = 4

        def swiglu(x, w1, w2, w3):
            return jax.nn.silu(x @ w1) * (x @ w3) @ w2
        B, S, D = x.shape
        E = Wg.shape[1]
        T = B * S
        xf = x.reshape(T, D)
        scores = jax.nn.softmax(xf @ Wg, axis=-1)
        weights, indices = jax.lax.top_k(scores, TOP_K)
        P = T * TOP_K
        pair_expert = indices.reshape(-1)
        pair_token = jnp.repeat(jnp.arange(T), TOP_K)
        pair_weight = weights.reshape(-1).astype(xf.dtype)
        C = CAP_FACTOR * P // E
        y = jnp.zeros_like(xf)
        for e in range(E):
            pos = jnp.nonzero(pair_expert == e, size=C, fill_value=P)[0]
            valid = pos < P
            safe = jnp.minimum(pos, P - 1)
            tok = jnp.where(valid, pair_token[safe], 0)
            w = jnp.where(valid, pair_weight[safe], 0.0)
            xg = xf[tok]
            out = swiglu(xg, W1[e], W2[e], W3[e]) * w[:, None]
            y = y.at[tok].add(out)
        z = swiglu(xf, Ws1, Ws2, Ws3)
        return (y + z).reshape(B, S, D)
    x = L0_attn_x
    xn = _layernorm(x, axis=-1)
    x = x + _L0_attn_ref(xn, L0_attn_Wg, L0_attn_bg, L0_attn_Wv, L0_attn_bv, L0_attn_Wo, L0_attn_bo) + _L0_ffn_ref(xn, L0_ffn_Wg, L0_ffn_W1, L0_ffn_W2, L0_ffn_W3, L0_ffn_Ws1, L0_ffn_Ws2, L0_ffn_Ws3)
    return x

_drawn_inputs = setup_inputs


def setup_inputs(seed=0):
    import zlib

    import numpy as np

    out = dict(_drawn_inputs(seed))
    spreads = {}
    factors = {'L0_attn_Wg': 8.0, 'L0_attn_bg': 8.0, 'L0_attn_bv': 6.902, 'L0_attn_bo': 6.29}
    for name, (base, spread) in spreads.items():
        noise = np.random.default_rng([zlib.crc32(name.encode()), seed]).standard_normal(out[name].shape)
        drawn = base * np.exp(spread * noise) if base else spread * noise
        out[name] = jnp.asarray(drawn.astype(out[name].dtype))
    for name, factor in factors.items():
        out[name] = (out[name] * factor).astype(out[name].dtype)
    return out
```

```python
import numpy as np
import concourse.bass as bass
from concourse import mybir
from contextlib import ExitStack

P = 128


def windowed_attention_and_routed_experts(nc, tokens_in, project_in, bias_in, out_bias_in, attn_out_in,
                                          up_in, down_in, tokens_out):
    f32, f32r = mybir.dt.float32, mybir.dt.float32r
    ALU = mybir.AluOpType
    ACT = mybir.ActivationFunctionType
    AX = mybir.AxisListType

    TILES = tokens_in.shape[1]
    D = tokens_in.shape[2]
    HEADS, HD = 16, 8
    SEQ_TILES = 2
    BANDS = SEQ_TILES + 1
    EXPERTS = 32
    TOP = 4
    PAIRS = up_in.shape[1]
    CHUNK_TILES = 4
    CHUNK = CHUNK_TILES * P
    CHUNKS = TILES // CHUNK_TILES
    SEQS = CHUNK_TILES // SEQ_TILES
    QUAD = 4
    GROUPS = SEQS * HEADS // QUAD
    CHUNK_HEADS = GROUPS * QUAD
    GPS = GROUPS // SEQS
    SLOTS = 32
    TERMS = 3 * HD
    CAPACITY = 4 * (TILES * P * TOP) // EXPERTS
    SEQ = SEQ_TILES * P
    LN_EPS, CORR_EPS = 1e-5, 1e-8
    G_RING, L_RING, T_RING, ACT_RING = 4, 2, 4, 3
    PROJ = project_in.shape[1]

    ctx = ExitStack()
    with ctx:
        def sb(name, shape, dt=f32):
            return ctx.enter_context(nc.sbuf_tensor(name, shape, dt))

        def pb(name):
            return ctx.enter_context(nc.psum_tensor(name, [P, 512], f32))

        def sem(name):
            return ctx.enter_context(nc.semaphore(name))

        class Count:

            def __init__(self, name, per):
                self.sem, self.per = sem(name), per

            def after(self, c, k):
                return c * self.per + (self.per + k + 1)

        x = sb("x", [P, TILES, D])
        xn = sb("xn", [P, TILES, D])
        xT = sb("xT", [P, TILES * P])
        x_hi = sb("x_hi", [P, TILES * P], f32r)
        x_lo = sb("x_lo", [P, TILES * P], f32r)
        up_hi = sb("up_hi", [P, PAIRS, 2, P], f32r)
        up_lo = sb("up_lo", [P, PAIRS, 2, P], f32r)
        UP_PIECES = 1 if PAIRS < 4 else 4
        up_bounds = [PAIRS * i // UP_PIECES for i in range(UP_PIECES + 1)]
        STAGE = max(b - a for a, b in zip(up_bounds, up_bounds[1:]))
        up_stage = sb("up_stage", [P, 2, STAGE, 2, P])
        down_w = sb("down_w", [P, PAIRS, D])
        proj_w = sb("proj_w", [P, PROJ])
        proj_b = sb("proj_b", [P, 2 * D])
        wo = sb("wo", [P, D])
        wo_b = sb("wo_b", [P, D])
        genes = sb("genes", [P, TILES, D])
        values = sb("values", [P, TILES, D])
        g_hi = sb("g_hi", [P, TILES, D], f32r)
        g_lo = sb("g_lo", [P, TILES, D])
        half_log = sb("half_log", [P, TILES, HEADS])
        gates = sb("gates", [P, TILES, EXPERTS])
        ident = sb("ident", [P, P])
        ones = sb("ones", [P, P])
        causal = sb("causal", [P, P])
        behind = sb("behind", [P, P])
        y_sb = sb("y_sb", [P, CHUNK])
        turned = y_sb
        turned_log = sb("turned_log", [P, 2 * P])

        pairs_tm = sb("pairs_tm", [P, SEQ_TILES, 2, HEADS, SLOTS])
        v32 = [sb(f"v32_{s}", [P, SEQ_TILES, HEADS, SLOTS]) for s in range(SEQS)]
        key_log = [sb(f"key_log{s}", [P, SEQ_TILES, HEADS]) for s in range(SEQS)]
        def room(buf, at, rows, cols):
            flat = buf[:, :, :].rearrange("p a b -> p (a b)")
            return flat[:, at * CHUNK:at * CHUNK + rows * cols].rearrange("p (a b) -> p a b", b=cols)

        pairs_T = [sb(f"pairs_T{i}", [P, 2, SEQ], f32r) for i in range(2)]
        row_log = [sb(f"row_log{i}", [P, SEQ_TILES, QUAD, P]) for i in range(L_RING)]
        damp = [sb(f"damp{i}", [P, BANDS, P]) for i in range(T_RING)]
        corr = [sb(f"corr{i}", [P, QUAD, BANDS * P]) for i in range(2)]
        corr2 = [sb("corr2_0", [P, QUAD, BANDS * P]), room(genes, 0, QUAD, BANDS * P)]
        mixed = room(xn, 0, 2, SEQ_TILES * P)
        sums = [sb(f"sums{s}", [P, 2, SEQ_TILES, HEADS, HD + 1]) for s in range(SEQS)]
        plain = [sb(f"plain{s}", [P, SEQ_TILES, HEADS, HD + 1]) for s in range(SEQS)]
        inv = sb("inv", [P, SEQ_TILES, HEADS])
        mean_d = sb("mean_d", [P, SEQ_TILES, HEADS])
        total = sb("total", [P, HEADS])
        alpha = sb("alpha", [P, SEQ_TILES, HEADS])
        num = sb("num", [P, SEQ_TILES, HEADS, HD + 1])
        num2 = sb("num2", [P, SEQ_TILES, HEADS, HD + 1])
        inv_sum = sb("inv_sum", [P, SEQ_TILES, HEADS])
        attended = sb("attended", [P, SEQ_TILES, D])
        attended_T = sb("attended_T", [P, SEQ])
        stage_flat = up_stage[:, :, :, :, :].rearrange("p i a b c -> p (i a b c)")
        gate_row = [stage_flat[:, i * CHUNK:(i + 1) * CHUNK] for i in range(G_RING)]
        silu = [xT[:, i * CHUNK:(i + 1) * CHUNK] for i in range(2)]
        glu = [xT[:, i * CHUNK:(i + 1) * CHUNK] for i in range(2, 4)]
        hidden = [room(xn, i + 1, 1, CHUNK)[:, 0, :] for i in range(ACT_RING)]

        stats = sb("stats", [P, TILES, 6])
        moments = sb("moments", [P, TILES, 2])
        var_eps = sb("var_eps", [P, TILES])
        std = sb("std", [P, TILES])
        rstd = sb("rstd", [P, TILES])
        newton = sb("newton", [P, TILES])
        norm2 = sb("norm2", [P, TILES, HEADS])
        norm = sb("norm", [P, TILES, HEADS])
        log_norm = sb("log_norm", [P, TILES, HEADS])
        logits = sb("logits", [P, TILES, EXPERTS])
        top8 = sb("top8", [P, TILES, 8])
        per_tile = [sb(f"per_tile{i}", [P, TILES]) for i in range(3)]

        squares = xn
        c_flat = corr[0][:, :, :].rearrange("p a b -> p (a b)")
        d_flat = corr2[0][:, :, :].rearrange("p a b -> p (a b)")
        prob, above, equal = (c_flat[:, i * 512:(i + 1) * 512].rearrange("p (t e) -> p t e", e=EXPERTS)
                              for i in range(3))
        ranked, place, chosen = (d_flat[:, i * 512:(i + 1) * 512].rearrange("p (t e) -> p t e", e=EXPERTS)
                                 for i in range(3))
        e_flat = corr[1][:, :, :].rearrange("p a b -> p (a b)")
        by_expert = e_flat[:, 0:512].rearrange("p (e t) -> p e t", t=TILES)
        carried = e_flat[:, 512:1024].rearrange("p (e t) -> p e t", t=TILES)
        f_flat = corr2[1][:, :, :].rearrange("p a b -> p (a b)")
        fresh_row = f_flat[:, 0:512].rearrange("p (t e) -> p t e", e=EXPERTS)
        fresh_expert = f_flat[:, 512:1024].rearrange("p (e t) -> p e t", t=TILES)

        H1, H3, Y, S0, S1, U, TA, TB = (pb(n) for n in ("H1", "H3", "Y", "S0", "S1", "U", "TA", "TB"))
        S = [S0, S1]

        gates_dram = nc.dram_tensor("gates_dram", (EXPERTS, TILES * P), f32, kind="Internal").ap()
        logs_dram = nc.dram_tensor("logs_dram", (TILES, HEADS, P), f32, kind="Internal").ap()

        steps = []

        def add(kind, k, n):
            if 0 <= k < n:
                steps.append((kind, k))

        HALF = CHUNK_HEADS // 2
        LAST = HALF + 8
        DENSE = 12
        pair_at = [[] for _ in range(LAST)]
        for p in range(PAIRS):
            pair_at[min(p * HALF // DENSE if p < DENSE else HALF + (p - DENSE), LAST - 1)].append(p)
        for t in range(-1, LAST):
            if t == -1:
                add("build", 0, SEQS)
                add("pair_turn", 0, GROUPS)
                for k in (0, 1):
                    add("damp", k, CHUNK_HEADS)
                continue
            for p in pair_at[t]:
                add("up", p, PAIRS)
                add("gate", p - 1, PAIRS)
            for s in range(SEQS):
                if t == (s + 1) * GPS * 2 + 4:
                    add("weigh", s, SEQS)
            if t % 2 == 0:
                g = t // 2
                add("mix_turn", g - 2, GROUPS)
                add("pair_turn", g + 1, GROUPS)
            add("score", 2 * t, CHUNK_HEADS)
            add("damp", 2 * t + 2, CHUNK_HEADS)
            for p in pair_at[t]:
                add("down", p - 2, PAIRS)
            add("score", 2 * t + 1, CHUNK_HEADS)
            add("damp", 2 * t + 3, CHUNK_HEADS)
            if t % 2 == 0:
                add("mix", t // 2 - 1, GROUPS)
            for s in range(SEQS):
                end = (s + 1) * GPS * 2
                if s >= 1 and t == end - GPS * 2 - 4:
                    add("build", s, SEQS)
                if t == end - GPS * 2 + 1:
                    add("plain", s, SEQS)
                if t == end + 3:
                    add("fit", s, SEQS)
                if t == end + 6:
                    add("attend", s, SEQS)
                if t == end + 7:
                    add("add_attended", s, SEQS)
        add("gate", PAIRS - 1, PAIRS)
        add("down", PAIRS - 2, PAIRS)
        add("down", PAIRS - 1, PAIRS)
        add("finish", 0, 1)
        for kind, n in (("pair_turn", GROUPS), ("mix", GROUPS), ("mix_turn", GROUPS), ("score", CHUNK_HEADS),
                        ("damp", CHUNK_HEADS), ("up", PAIRS), ("down", PAIRS), ("fit", SEQS), ("weigh", SEQS),
                        ("plain", SEQS), ("attend", SEQS), ("add_attended", SEQS)):
            assert [k for what, k in steps if what == kind] == list(range(n)), kind

        tb_uses = []
        for kind, k in steps:
            if kind in ("mix_turn", "plain", "fit", "finish"):
                tb_uses.append((kind, k))
            if kind == "attend":
                tb_uses += [("attend", k), ("add_attended", k)]

        x_in = [sem(f"x_in{i}") for i in range(CHUNKS)]
        proj_in, consts_in, wo_in, down_ld = sem("proj_in"), sem("consts_in"), sem("wo_in"), sem("down_ld")
        up_ld = [sem(f"up_ld{i}") for i in range(2)]
        up_hi_done, up_lo_done = sem("up_hi_done"), sem("up_lo_done")
        made = sem("made")
        filled = sem("filled")
        v_step = sem("v_step")
        var_ready, std_ready = sem("var_ready"), sem("std_ready")
        xn_ready, xT_turned, xT_kept, x_split = sem("xn_ready"), sem("xT_turned"), sem("xT_kept"), sem("x_split")
        projected, genes_kept, logits_kept = sem("projected"), sem("genes_kept"), sem("logits_kept")
        squared, norm2_ready, norm_ready, clamped, logged = (sem(n) for n in (
            "squared", "norm2_ready", "norm_ready", "clamped", "logged"))
        shifted, prob_ready, chosen_ready, counted, gates_ready = (sem(n) for n in (
            "shifted", "prob_ready", "chosen_ready", "counted", "gates_ready"))
        half_ready, genes_ready, bias_added = sem("half_ready"), sem("genes_ready"), sem("bias_added")
        gates_turned, gates_kept, logs_turned, logs_kept = (sem(n) for n in (
            "gates_turned", "gates_kept", "logs_turned", "logs_kept"))
        gates_stored, logs_stored = sem("gates_stored"), sem("logs_stored")
        gate_ld = [sem(f"gate_ld{i}") for i in range(G_RING)]
        log_ld = [sem(f"log_ld{i}") for i in range(L_RING)]
        stored, let_on = sem("stored"), sem("let_on")

        built = Count("built", SEQS)
        pair_turned, pair_kept = Count("pair_turned", GROUPS), Count("pair_kept", GROUPS)
        scored, damped = Count("scored", CHUNK_HEADS), Count("damped", CHUNK_HEADS)
        windowed, correlated = Count("windowed", CHUNK_HEADS), Count("correlated", CHUNK_HEADS)
        squared2 = Count("squared2", CHUNK_HEADS)
        mix_done, mix_kept = Count("mix_done", GROUPS), Count("mix_kept", GROUPS)
        tb_written, tb_read = Count("tb_written", len(tb_uses)), Count("tb_read", len(tb_uses))
        fitted, attended_ready = Count("fitted", SEQS), Count("attended_ready", SEQS)
        NORM_STEPS = 8
        norm_step = Count("norm_step", NORM_STEPS * SEQS)
        up1_done, up3_done = Count("up1_done", PAIRS), Count("up3_done", PAIRS)
        silu_done, glu_done = Count("silu_done", PAIRS), Count("glu_done", PAIRS)
        gated_done, down_done = Count("gated_done", PAIRS - 1), Count("down_done", PAIRS)
        y_kept, summed = Count("y_kept", 1), Count("summed", 1)

        def last_use(k, ring, per):
            return next(j for j in range(k - 1, k - 1 - per, -1) if (j % per) % ring == k % ring)

        def tb(kind, k):
            return tb_uses.index((kind, k))

        block = ctx.enter_context(nc.Block())

        @block.sync
        def _(sp):
            for c in range(CHUNKS):
                q = slice(c * CHUNK_TILES, (c + 1) * CHUNK_TILES)
                sp.dma_start(x[:, q, :], tokens_in[:, q, :]).then_inc(x_in[c], 16)
            sp.dma_start(proj_w[:, :], project_in).then_inc(proj_in, 16)
            sp.dma_start(proj_b[:, :], bias_in.partition_broadcast(P)).then_inc(consts_in, 16)
            sp.dma_start(wo_b[:, :], out_bias_in.partition_broadcast(P)).then_inc(consts_in, 16)
            for i in range(UP_PIECES):
                a, b = up_bounds[i], up_bounds[i + 1]
                if i >= 2:
                    sp.wait_ge(up_lo_done, i - 1)
                sp.dma_start(up_stage[:, i % 2, 0:b - a, :, :], up_in[:, a:b, :, :]).then_inc(up_ld[i % 2], 16)
            sp.dma_start(down_w[:, :, :], down_in).then_inc(down_ld, 16)
            sp.dma_start(wo[:, :], attn_out_in).then_inc(wo_in, 16)

            sp.wait_ge(logs_kept, 1)
            for i in range(2):
                rows = logs_dram.rearrange("t h p -> (t h) p")[i * P:(i + 1) * P, :]
                sp.dma_start(rows, turned_log[:, i * P:(i + 1) * P]).then_inc(logs_stored, 16)
            sp.wait_ge(gates_kept, 1)
            for t in range(TILES):
                part = (t % 4) * EXPERTS
                sp.dma_start(gates_dram[:, t * P:(t + 1) * P],
                             turned[part:part + EXPERTS, (t // 4) * P:(t // 4 + 1) * P]).then_inc(gates_stored, 16)
            sp.wait_ge(logs_stored, 32)
            sp.wait_ge(gates_stored, 16 * TILES)

            sp.wait_ge(up_lo_done, UP_PIECES)

            with sp.Fori(0, CHUNKS) as c:
                for kind, k in steps:
                    if kind == "damp" and k % QUAD == 0:
                        g = k // QUAD
                        s, q = g // GPS, g % GPS
                        sp.wait_ge(damped.sem, damped.after(c, QUAD * (g - L_RING) + QUAD - 1))
                        src = logs_dram[bass.ds(c * CHUNK_TILES + s * SEQ_TILES, SEQ_TILES),
                                        q * QUAD:(q + 1) * QUAD, :]
                        sp.dma_start(row_log[g % L_RING][:, :, :, :],
                                     src.partition_broadcast(P)).then_inc(log_ld[g % L_RING], 16)
                    if kind == "up" and k >= 1:
                        slot = (k - 1) % G_RING
                        sp.wait_ge(gated_done.sem, gated_done.after(c, k - 1 - G_RING))
                        for half in range(2):
                            row = gates_dram[2 * (k - 1) + half, bass.ds(c * CHUNK, CHUNK)]
                            sp.dma_start(gate_row[slot][half * 64:(half + 1) * 64, :],
                                         row.partition_broadcast(64)).then_inc(gate_ld[slot], 16)
                sp.wait_ge(summed.sem, summed.after(c, 0))
                sp.dma_start(tokens_out[:, bass.ds(c * CHUNK_TILES, CHUNK_TILES), :],
                             x[:, bass.ds(c * CHUNK_TILES, CHUNK_TILES), :]).then_inc(stored, 16)
            sp.wait_ge(stored, 16 * CHUNKS)

        @block.gpsimd
        def _(pool):
            n = [0]

            def chain(ins):
                n[0] += 1
                ins.then_inc(filled, 1)
                pool.wait_ge(filled, n[0])

            chain(nc.gpsimd.memset(ident[:, :], 0.0))
            nc.gpsimd.affine_select(out=ident[:, :], in_=ident[:, :], compare_op=ALU.not_equal, fill=1.0, base=0,
                                    pattern=[[-1, P]], channel_multiplier=1).then_inc(made, 1)
            chain(nc.gpsimd.memset(ones[:, :], 1.0))
            nc.gpsimd.affine_select(out=causal[:, :], in_=ones[:, :], compare_op=ALU.is_ge, fill=0.0, base=0,
                                    pattern=[[1, P]], channel_multiplier=-1).then_inc(made, 1)
            nc.gpsimd.affine_select(out=behind[:, :], in_=ones[:, :], compare_op=ALU.is_ge, fill=0.0, base=0,
                                    pattern=[[-1, P]], channel_multiplier=1).then_inc(made, 1)
            nc.gpsimd.memset(pairs_tm[:, :, :, :, :], 0.0).then_inc(filled, 1)
            n[0] += 1
            for s in range(SEQS):
                nc.gpsimd.memset(v32[s][:, :, :, :], 0.0).then_inc(filled, 1)
                n[0] += 1
            pool.wait_ge(filled, n[0])
            for s in range(SEQS):
                ins = nc.gpsimd.memset(v32[s][:, :, :, HD:HD + 1], 1.0)
                n[0] += 1
                ins.then_inc(filled, 1)
            for i in range(UP_PIECES):
                a, b = up_bounds[i], up_bounds[i + 1]
                pool.wait_ge(up_hi_done, i + 1)
                nc.gpsimd.tensor_tensor(up_lo[:, a:b, :, :], up_stage[:, i % 2, 0:b - a, :, :],
                                        up_hi[:, a:b, :, :].bitcast(f32), ALU.subtract).then_inc(up_lo_done, 1)

            for count in (built, windowed, gated_done):
                pool.sem_inc(count.sem, count.per)
            pool.wait_ge(filled, n[0])
            pool.wait_ge(genes_ready, 1)
            pool.wait_ge(half_ready, 1)
            outside = pool.to_reg(-1.0)

            def go():
                pool.sem_inc(let_on, 1)

            with pool.Fori(0, CHUNKS) as c:
                for kind, k in steps:
                    if kind == "build":
                        s = k
                        rows = bass.ds(c * CHUNK_TILES + s * SEQ_TILES, SEQ_TILES)
                        pool.wait_ge(pair_turned.sem, pair_turned.after(c, s * GPS - 1))
                        pool.wait_ge(mix_done.sem, mix_done.after(c, (s + 1) * GPS - 1 - GROUPS))
                        pool.wait_ge(damped.sem, damped.after(c, (s + 1) * GPS * QUAD - 1 - CHUNK_HEADS))
                        go()

                        def part(which, at):
                            return pairs_tm[:, :, which, :, at * HD:(at + 1) * HD]

                        hi = g_hi[:, rows, :].bitcast(f32).rearrange("p t (h d) -> p t h d", d=HD)
                        lo = g_lo[:, rows, :].rearrange("p t (h d) -> p t h d", d=HD)
                        vals = values[:, rows, :].rearrange("p t (h d) -> p t h d", d=HD)
                        for dst, src in ((part(0, 0), hi), (part(0, 1), lo), (part(0, 2), hi),
                                         (part(1, 0), hi), (part(1, 1), hi), (part(1, 2), lo),
                                         (v32[s][:, :, :, 0:HD], vals)):
                            nc.gpsimd.tensor_copy(dst, src)
                        nc.gpsimd.tensor_copy(key_log[s][:, :, :], half_log[:, rows, :]).then_inc(built.sem, 1)
                    if kind == "damp":
                        pool.wait_ge(damped.sem, damped.after(c, k))
                        go()
                        t = damp[k % T_RING]
                        nc.gpsimd.affine_select(out=t[:, 0:3:2, :], in_=t[:, 0:3:2, :], compare_op=ALU.is_ge,
                                                fill=outside, base=0, pattern=[[0, 2], [1, P]], channel_multiplier=-1)
                        nc.gpsimd.affine_select(out=t[:, 1, :], in_=t[:, 1, :], compare_op=ALU.is_ge,
                                                fill=outside, base=0, pattern=[[-1, P]],
                                                channel_multiplier=1).then_inc(windowed.sem, 1)
                    if kind == "gate" and k >= 1:
                        slot = (k - 1) % G_RING
                        uses = (PAIRS - 1) // G_RING
                        pool.wait_ge(glu_done.sem, glu_done.after(c, k))
                        pool.wait_ge(gate_ld[slot], c * (32 * uses) + 32 * ((k - 1) // G_RING + 1))
                        pool.wait_ge(down_done.sem, down_done.after(c, last_use(k, ACT_RING, PAIRS)))
                        nc.gpsimd.tensor_tensor(hidden[k % ACT_RING][:, :], glu[k % 2][:, :],
                                                gate_row[slot][:, :], ALU.mult).then_inc(gated_done.sem, 1)

        @block.scalar
        def _(act):
            act.wait_ge(var_ready, 1)
            nc.scalar.activation(std[:, :], var_eps[:, :], ACT.Sqrt).then_inc(std_ready, 1)
            for q in range(CHUNKS):
                act.wait_ge(xT_turned, q + 1)
                nc.scalar.activation(xT[:, q * CHUNK:(q + 1) * CHUNK], S[q % 2][:, :], ACT.Copy).then_inc(xT_kept, 1)
            for q in range(2):
                act.wait_ge(genes_kept, (q + 1) * TILES // 2)
                r = slice(q * TILES // 2, (q + 1) * TILES // 2)
                nc.scalar.activation(squares[:, r, :], genes[:, r, :], ACT.Square).then_inc(squared, 1)
            act.wait_ge(norm2_ready, 1)
            nc.scalar.activation(norm[:, :, :], norm2[:, :, :], ACT.Sqrt).then_inc(norm_ready, 1)
            act.wait_ge(clamped, 1)
            nc.scalar.activation(log_norm[:, :, :], norm[:, :, :], ACT.Ln, scale=CORR_EPS ** -0.5).then_inc(logged, 1)
            act.wait_ge(shifted, 1)
            nc.scalar.activation(prob, logits[:, :, :], ACT.Exp).then_inc(prob_ready, 1)
            for i in range(UP_PIECES):
                a, b = up_bounds[i], up_bounds[i + 1]
                act.wait_ge(up_ld[i % 2], 16 * (i // 2 + 1))
                nc.scalar.activation(up_hi[:, a:b, :, :], up_stage[:, i % 2, 0:b - a, :, :],
                                     ACT.Copy).then_inc(up_hi_done, 1)
            act.wait_ge(logs_turned, 1)
            nc.scalar.activation(turned_log[:, :], TB[:, 0:2 * P], ACT.Copy).then_inc(logs_kept, 1)
            act.wait_ge(gates_turned, 1)
            nc.scalar.activation(turned[:, :], TA[:, :], ACT.Copy).then_inc(gates_kept, 1)

            for count in (damped, squared2, pair_kept, mix_kept, silu_done, y_kept):
                act.sem_inc(count.sem, count.per)
            with act.Fori(0, CHUNKS) as c:
                def keep_pairs(g):
                    act.wait_ge(pair_turned.sem, pair_turned.after(c, g))
                    act.wait_ge(scored.sem, scored.after(c, QUAD * (g - 2) + QUAD - 1))
                    nc.scalar.activation(pairs_T[g % 2][:, :, :], TA[:, :].rearrange("p (w q) -> p w q", w=2),
                                         ACT.Copy).then_inc(pair_kept.sem, 1)

                def square(k):
                    g, h = k // QUAD, k % QUAD
                    act.wait_ge(correlated.sem, correlated.after(c, k))
                    act.wait_ge(mix_done.sem, mix_done.after(c, g - 2))
                    nc.scalar.activation(corr2[g % 2][:, h, :], corr[g % 2][:, h, :], ACT.Square,
                                         scale=0.5).then_inc(squared2.sem, 1)

                for kind, k in steps:
                    if kind == "pair_turn":
                        keep_pairs(k)
                    if kind == "damp":
                        g, h = k // QUAD, k % QUAD
                        s = g // GPS
                        if h == 0:
                            act.wait_ge(log_ld[g % L_RING], c * (16 * GROUPS // L_RING) + 16 * (g // L_RING + 1))
                            act.wait_ge(built.sem, built.after(c, s))
                        act.wait_ge(correlated.sem, correlated.after(c, k - T_RING))
                        head = (g % GPS) * QUAD + h
                        rows = row_log[g % L_RING]
                        nc.scalar.activation(damp[k % T_RING][:, 0:2, :], rows[:, :, h, :], ACT.Tanh,
                                             bias=key_log[s][:, 0, head:head + 1])
                        nc.scalar.activation(damp[k % T_RING][:, 2, :], rows[:, 1, h, :], ACT.Tanh,
                                             bias=key_log[s][:, 1, head:head + 1]).then_inc(damped.sem, 1)
                    if kind == "score" and k >= 1:
                        square(k - 1)
                    if kind == "score" and k == CHUNK_HEADS - 1:
                        square(k)
                    if kind == "mix":
                        act.wait_ge(mix_done.sem, mix_done.after(c, k))
                        act.wait_ge(tb_written.sem, tb_written.after(
                            c, tb("mix_turn", k - 1) if k else tb("mix_turn", GROUPS - 1) - len(tb_uses)))
                        nc.scalar.activation(mixed[:, :, :].rearrange("p a b -> p (a b)"), U[:, :],
                                             ACT.Copy).then_inc(mix_kept.sem, 1)
                    if kind == "plain":
                        act.wait_ge(tb_written.sem, tb_written.after(c, tb("plain", k)))
                        act.wait_ge(norm_step.sem, norm_step.after(c, NORM_STEPS * (k + 1) - 1 - NORM_STEPS * SEQS))
                        nc.scalar.activation(plain[k][:, :, :, :].rearrange("p a b c -> p (a b c)"),
                                             TB[:, 0:SEQ_TILES * HEADS * (HD + 1)],
                                             ACT.Copy).then_inc(tb_read.sem, 1)
                    if kind == "up":
                        act.wait_ge(up1_done.sem, up1_done.after(c, k))
                        act.wait_ge(glu_done.sem, glu_done.after(c, last_use(k, 2, PAIRS)))
                        nc.scalar.activation(silu[k % 2][:, :], H1[:, :], ACT.Silu).then_inc(silu_done.sem, 1)
                    if kind == "attend":
                        act.wait_ge(tb_written.sem, tb_written.after(c, tb("attend", k)))
                        nc.scalar.activation(attended_T[:, :], TB[:, 0:SEQ], ACT.Copy).then_inc(tb_read.sem, 1)
                    if kind == "finish":
                        act.wait_ge(down_done.sem, down_done.after(c, PAIRS - 1))
                        act.wait_ge(tb_written.sem, tb_written.after(c, tb("finish", 0) - len(tb_uses)))
                        nc.scalar.activation(y_sb[:, :], Y[:, :], ACT.Copy).then_inc(y_kept.sem, 1)

        @block.vector
        def _(dve):
            n = [0]

            def chain(ins):
                n[0] += 1
                ins.then_inc(v_step, 1)
                dve.wait_ge(v_step, n[0])

            for q in range(CHUNKS):
                dve.wait_ge(x_in[q], 16)
                for t in range(q * CHUNK_TILES, (q + 1) * CHUNK_TILES):
                    last = nc.vector.bn_stats(stats[:, t, :], x[:, t, :])
            chain(last)
            for t in range(TILES):
                last = nc.vector.bn_aggr(moments[:, t, :], stats[:, t, :])
            chain(last)
            nc.vector.tensor_scalar(var_eps[:, :], moments[:, :, 1], LN_EPS, None, ALU.add).then_inc(var_ready, 1)
            dve.wait_ge(std_ready, 1)
            chain(nc.vector.reciprocal(rstd[:, :], std[:, :]))
            chain(nc.vector.tensor_tensor(newton[:, :], rstd[:, :], rstd[:, :], ALU.mult))
            dve.wait_ge(var_ready, 1)
            chain(nc.vector.tensor_tensor(newton[:, :], newton[:, :], var_eps[:, :], ALU.mult))
            chain(nc.vector.tensor_scalar(newton[:, :], newton[:, :], -0.5, 1.5, ALU.mult, ALU.add))
            chain(nc.vector.tensor_tensor(rstd[:, :], rstd[:, :], newton[:, :], ALU.mult))
            for t in range(TILES):
                nc.vector.tensor_scalar(xn[:, t, :], x[:, t, :], moments[:, t, 0:1], rstd[:, t:t + 1],
                                        ALU.subtract, ALU.mult).then_inc(xn_ready, 1)
            dve.wait_ge(consts_in, 32)
            dve.wait_ge(xn_ready, TILES)
            nc.vector.tensor_tensor(x[:, :, :], x[:, :, :], wo_b[:, :].unsqueeze(1).to_broadcast([P, TILES, D]),
                                    ALU.add).then_inc(bias_added, 1)
            for q in range(CHUNKS):
                cols = slice(q * CHUNK, (q + 1) * CHUNK)
                for t in range(q * CHUNK_TILES, (q + 1) * CHUNK_TILES):
                    dve.wait_ge(projected, t + 1)
                    bank = (H1, H3)[t % 2]
                    nc.vector.tensor_copy(logits[:, t, :], bank[:, 2 * D:PROJ]).then_inc(logits_kept, 1)
                    nc.vector.tensor_tensor(genes[:, t, :], bank[:, 0:D], proj_b[:, 0:D], ALU.add)
                    nc.vector.tensor_tensor(values[:, t, :], bank[:, D:2 * D], proj_b[:, D:2 * D],
                                            ALU.add).then_inc(genes_kept, 1)

            for q in range(2):
                dve.wait_ge(squared, q + 1)
                r = slice(q * TILES // 2, (q + 1) * TILES // 2)
                last = nc.vector.tensor_reduce(norm2[:, r, :], squares[:, r, :].rearrange("p t (h d) -> p t h d", d=HD),
                                               AX.X, ALU.add)
            last.then_inc(norm2_ready, 1)
            dve.wait_ge(norm_ready, 1)
            nc.vector.tensor_scalar(norm[:, :, :], norm[:, :, :], 1e-22, 1e14, ALU.max, ALU.min).then_inc(clamped, 1)
            dve.wait_ge(clamped, 1)
            chain(nc.vector.reciprocal(norm2[:, :, :], norm[:, :, :]))
            unit = xn
            inv_b = norm2[:, :, :].unsqueeze(3).to_broadcast([P, TILES, HEADS, HD])
            chain(nc.vector.tensor_tensor(unit[:, :, :].rearrange("p t (h d) -> p t h d", d=HD),
                                          genes[:, :, :].rearrange("p t (h d) -> p t h d", d=HD), inv_b, ALU.mult))
            chain(nc.vector.tensor_scalar(g_lo[:, :, :], unit[:, :, :], 0.0, 1.0, ALU.max, ALU.min))
            chain(nc.vector.tensor_scalar(unit[:, :, :], unit[:, :, :], 0.0, -1.0, ALU.min, ALU.max))
            chain(nc.vector.tensor_tensor(unit[:, :, :], unit[:, :, :], g_lo[:, :, :], ALU.add))
            chain(nc.vector.tensor_copy(g_hi[:, :, :], unit[:, :, :]))
            nc.vector.tensor_tensor(g_lo[:, :, :], unit[:, :, :], g_hi[:, :, :].bitcast(f32),
                                    ALU.subtract).then_inc(genes_ready, 1)
            dve.wait_ge(logged, 1)
            nc.vector.tensor_scalar(half_log[:, :, :], log_norm[:, :, :], 0.5, None, ALU.mult).then_inc(half_ready, 1)

            dve.wait_ge(logits_kept, TILES)
            top_b = per_tile[0][:, :].unsqueeze(2).to_broadcast([P, TILES, EXPERTS])
            chain(nc.vector.tensor_reduce(per_tile[0][:, :], logits[:, :, :], AX.X, ALU.max))
            chain(nc.vector.tensor_tensor(logits[:, :, :], logits[:, :, :], top_b, ALU.subtract))
            nc.vector.tensor_scalar(logits[:, :, :], logits[:, :, :], -87.33, None, ALU.max).then_inc(shifted, 1)
            dve.wait_ge(shifted, 1)
            for t in range(TILES):
                last = nc.vector.max(top8[:, t, :], logits[:, t, :])
            chain(last)
            fourth = top8[:, :, TOP - 1:TOP].to_broadcast([P, TILES, EXPERTS])
            nc.vector.tensor_tensor(above, logits[:, :, :], fourth, ALU.is_gt)
            nc.vector.memset(fresh_row, 1.0)
            chain(nc.vector.memset(fresh_expert, 1.0))
            nc.vector.memset(fresh_row[:, :, 0:1], 0.0)
            nc.vector.memset(fresh_expert[:, :, 0:1], 0.0)
            chain(nc.vector.tensor_tensor(equal, logits[:, :, :], fourth, ALU.is_equal))
            chain(nc.vector.tensor_reduce(per_tile[1][:, :], above, AX.X, ALU.add))
            nc.vector.tensor_scalar(per_tile[1][:, :], per_tile[1][:, :], -1.0, float(TOP), ALU.mult, ALU.add)
            chain(nc.vector.tensor_tensor_scan(ranked.rearrange("p t e -> p (t e)"),
                                               fresh_row.rearrange("p t e -> p (t e)"),
                                               equal.rearrange("p t e -> p (t e)"), 0.0, ALU.mult, ALU.add))
            left_b = per_tile[1][:, :].unsqueeze(2).to_broadcast([P, TILES, EXPERTS])
            chain(nc.vector.tensor_tensor(ranked, ranked, left_b, ALU.is_le))
            chain(nc.vector.tensor_tensor(equal, equal, ranked, ALU.mult))
            nc.vector.tensor_tensor(chosen, equal, above, ALU.add).then_inc(chosen_ready, 1)
            dve.wait_ge(counted, 1)
            in_tile = S0[:, :].rearrange("p (t e) -> p t e", e=EXPERTS)
            per_expert = S1[:, :].rearrange("p (t e) -> p e t", e=EXPERTS)
            chain(nc.vector.tensor_copy(by_expert, per_expert))
            chain(nc.vector.tensor_tensor_scan(carried.rearrange("p e t -> p (e t)"),
                                               fresh_expert.rearrange("p e t -> p (e t)"),
                                               by_expert.rearrange("p e t -> p (e t)"), 0.0, ALU.mult, ALU.add))
            chain(nc.vector.tensor_tensor(carried, carried, by_expert, ALU.subtract))
            chain(nc.vector.tensor_tensor(place, in_tile, carried.rearrange("p e t -> p t e"), ALU.add))
            chain(nc.vector.tensor_scalar(place, place, float(CAPACITY), None, ALU.is_le))
            chain(nc.vector.tensor_tensor(place, place, chosen, ALU.mult))
            dve.wait_ge(prob_ready, 1)
            chain(nc.vector.tensor_reduce(per_tile[0][:, :], prob, AX.X, ALU.add))
            chain(nc.vector.reciprocal(per_tile[2][:, :], per_tile[0][:, :]))
            share_b = per_tile[2][:, :].unsqueeze(2).to_broadcast([P, TILES, EXPERTS])
            chain(nc.vector.tensor_tensor(above, prob, share_b, ALU.mult))
            nc.vector.tensor_tensor(gates[:, :, :], above, place, ALU.mult).then_inc(gates_ready, 1)
            for q in range(CHUNKS):
                cols = slice(q * CHUNK, (q + 1) * CHUNK)
                dve.wait_ge(xT_kept, q + 1)
                last = nc.vector.tensor_copy(x_hi[:, cols], xT[:, cols])
            chain(last)
            nc.vector.tensor_tensor(x_lo[:, :], xT[:, :], x_hi[:, :].bitcast(f32), ALU.subtract).then_inc(x_split, 1)

            for count in (correlated, glu_done, tb_read, fitted, attended_ready, norm_step, summed):
                dve.sem_inc(count.sem, count.per)
            with dve.Fori(0, CHUNKS) as c:
                for kind, k in steps:
                    if kind == "score":
                        g, h = k // QUAD, k % QUAD
                        dve.wait_ge(scored.sem, scored.after(c, k))
                        dve.wait_ge(windowed.sem, windowed.after(c, k))
                        dve.wait_ge(mix_done.sem, mix_done.after(c, g - 2))
                        nc.vector.scalar_tensor_tensor(
                            out=corr[g % 2][:, h, :], in0=damp[k % T_RING][:, :, :].rearrange("p a b -> p (a b)"),
                            scalar=1.0, in1=S[k % 2][:, 0:BANDS * P], op0=ALU.add,
                            op1=ALU.mult).then_inc(correlated.sem, 1)
                    if kind == "mix_turn":
                        dve.wait_ge(tb_written.sem, tb_written.after(c, tb("mix_turn", k)))
                        s, q = k // GPS, k % GPS
                        src = TB[:, :].rearrange("p (a h w) -> p a h w", h=QUAD, w=SLOTS)[:, :, :, 0:HD + 1]
                        dst = sums[s][:, :, :, q * QUAD:(q + 1) * QUAD, :].rearrange("p a b h w -> p (a b) h w")
                        nc.vector.tensor_copy(dst, src).then_inc(tb_read.sem, 1)
                    if kind == "up":
                        dve.wait_ge(up3_done.sem, up3_done.after(c, k))
                        dve.wait_ge(silu_done.sem, silu_done.after(c, k))
                        if k == 0:
                            dve.wait_ge(down_done.sem, down_done.after(c, last_use(k, ACT_RING, PAIRS)))
                            dst = hidden[0]
                        else:
                            dve.wait_ge(gated_done.sem, gated_done.after(c, k - 3))
                            dst = glu[k % 2]
                        nc.vector.tensor_tensor(dst[:, :], silu[k % 2][:, :], H3[:, :],
                                                ALU.mult).then_inc(glu_done.sem, 1)
                    first = NORM_STEPS * k

                    def own(j):
                        dve.wait_ge(norm_step.sem, norm_step.after(c, first + j))

                    if kind == "fit":
                        dve.wait_ge(tb_read.sem, tb_read.after(c, tb("mix_turn", (k + 1) * GPS - 1)))
                        nc.vector.tensor_scalar(mean_d[:, :, :], sums[k][:, 0, :, :, HD], 1.0 / (4 * SEQ), 1.0,
                                                ALU.mult, ALU.add).then_inc(norm_step.sem, 1)
                        own(0)
                        nc.vector.reciprocal(inv[:, :, :], mean_d[:, :, :]).then_inc(fitted.sem, 1)
                    if kind == "weigh":
                        dve.wait_ge(tb_written.sem, tb_written.after(c, tb("fit", k)))
                        nc.vector.reciprocal(total[:, :], TB[:, 0:HEADS]).then_inc(tb_read.sem, 1)
                        dve.wait_ge(tb_read.sem, tb_read.after(c, tb("fit", k)))
                        dve.wait_ge(fitted.sem, fitted.after(c, k))
                        nc.vector.scalar_tensor_tensor(
                            out=alpha[:, :, :], in0=inv[:, :, :], scalar=0.25,
                            in1=total[:, :].unsqueeze(1).to_broadcast([P, SEQ_TILES, HEADS]),
                            op0=ALU.mult, op1=ALU.mult).then_inc(norm_step.sem, 1)
                        own(1)
                        M = SEQ_TILES * HEADS
                        a_b = alpha[:, :, :].rearrange("p t h -> p (t h)").unsqueeze(2).to_broadcast([P, M, HD + 1])

                        def rows(buf):
                            return buf.rearrange("p t h w -> p (t h) w")

                        first_sum, second_sum = rows(sums[k][:, 0]), rows(sums[k][:, 1])
                        nc.vector.scalar_tensor_tensor(out=rows(num[:, :, :, :]), in0=second_sum, scalar=2.0, in1=a_b,
                                                       op0=ALU.mult, op1=ALU.mult).then_inc(norm_step.sem, 1)
                        own(2)
                        nc.vector.tensor_tensor(rows(num2[:, :, :, :]), rows(num[:, :, :, :]), first_sum,
                                                ALU.add).then_inc(norm_step.sem, 1)
                        own(3)
                        nc.vector.tensor_tensor(rows(num[:, :, :, :]), rows(num2[:, :, :, :]), a_b,
                                                ALU.mult).then_inc(norm_step.sem, 1)
                        own(4)
                        dve.wait_ge(tb_read.sem, tb_read.after(c, tb("plain", k)))
                        nc.vector.tensor_tensor(rows(num2[:, :, :, :]), rows(num[:, :, :, :]), rows(plain[k][:, :, :, :]),
                                                ALU.add).then_inc(norm_step.sem, 1)
                        own(5)
                        nc.vector.reciprocal(inv_sum[:, :, :], num2[:, :, :, HD]).then_inc(norm_step.sem, 1)
                        own(6)
                        dve.wait_ge(tb_written.sem, tb_written.after(
                            c, tb("attend", k - 1) if k else tb("attend", SEQS - 1) - len(tb_uses)))
                        nc.vector.tensor_tensor(
                            attended[:, :, :].rearrange("p t (h w) -> p (t h) w", w=HD),
                            rows(num2[:, :, :, 0:HD]),
                            inv_sum[:, :, :].rearrange("p t h -> p (t h)").unsqueeze(2).to_broadcast([P, M, HD]),
                            ALU.mult).then_inc(attended_ready.sem, 1)
                        dve.wait_ge(attended_ready.sem, attended_ready.after(c, k))
                        dve.sem_inc(norm_step.sem, 1)
                    if kind == "add_attended":
                        dve.wait_ge(tb_written.sem, tb_written.after(c, tb("add_attended", k)))
                        r = bass.ds(c * CHUNK_TILES + k * SEQ_TILES, SEQ_TILES)
                        nc.vector.tensor_tensor(x[:, r, :], TB[:, 0:SEQ_TILES * D].rearrange("p (t d) -> p t d", d=D),
                                                x[:, r, :], ALU.add).then_inc(tb_read.sem, 1)
                    if kind == "finish":
                        dve.wait_ge(tb_written.sem, tb_written.after(c, tb("finish", 0)))
                        dve.wait_ge(tb_read.sem, tb_read.after(c, tb("add_attended", SEQS - 1)))
                        r = bass.ds(c * CHUNK_TILES, CHUNK_TILES)
                        nc.vector.tensor_tensor(x[:, r, :], TB[:, :].rearrange("p (t d) -> p t d", d=D),
                                                x[:, r, :], ALU.add).then_inc(summed.sem, 1)
                        dve.wait_ge(summed.sem, summed.after(c, 0))
                        dve.sem_inc(tb_read.sem, 1)

        @block.tensor
        def _(pe):
            pe.wait_ge(made, 3)
            pe.wait_ge(proj_in, 16)
            for q in range(CHUNKS):
                if q >= 2:
                    pe.wait_ge(xT_kept, q - 1)
                for t in range(q * CHUNK_TILES, (q + 1) * CHUNK_TILES):
                    pe.wait_ge(xn_ready, t + 1)
                    j = t % CHUNK_TILES
                    last = nc.tensor.transpose(S[q % 2][:, j * P:(j + 1) * P], xn[:, t, :], ident[:, :])
                last.then_inc(xT_turned, 1)
                pe.wait_ge(xT_kept, q + 1)
                for t in range(q * CHUNK_TILES, (q + 1) * CHUNK_TILES):
                    if t >= 2:
                        pe.wait_ge(genes_kept, t - 1)
                    nc.tensor.matmul((H1, H3)[t % 2][:, 0:PROJ], xT[:, t * P:(t + 1) * P], proj_w[:, :],
                                     start=True, stop=True).then_inc(projected, 1)
            pe.wait_ge(half_ready, 1)
            for i in range(2):
                last = nc.tensor.transpose(TB[:, i * P:(i + 1) * P],
                                           half_log[:, 8 * i:8 * (i + 1), :].rearrange("p t h -> p (t h)"),
                                           ident[:, :])
            last.then_inc(logs_turned, 1)
            pe.wait_ge(chosen_ready, 1)
            flat = chosen.rearrange("p t e -> p (t e)")
            nc.tensor.matmul(S0[:, :], causal[:, :], flat, start=True, stop=True)
            nc.tensor.matmul(S1[:, :], ones[:, :], flat, start=True, stop=True).then_inc(counted, 1)
            pe.wait_ge(gates_ready, 1)
            for i in range(4):
                last = nc.tensor.transpose(TA[:, i * P:(i + 1) * P],
                                           gates[:, 4 * i:4 * (i + 1), :].rearrange("p t e -> p (t e)"), ident[:, :])
            last.then_inc(gates_turned, 1)
            pe.wait_ge(gates_kept, 1)
            pe.wait_ge(logs_kept, 1)
            pe.wait_ge(up_lo_done, UP_PIECES)
            pe.wait_ge(x_split, 1)
            pe.wait_ge(down_ld, 16)
            pe.wait_ge(wo_in, 16)

            for count in (pair_turned, scored, mix_done, tb_written, up1_done, up3_done, down_done):
                pe.sem_inc(count.sem, count.per)
            with pe.Fori(0, CHUNKS) as c:
                def take_tb(kind, k):
                    pe.wait_ge(tb_read.sem, tb_read.after(c, tb(kind, k) - 1))

                xs_hi, xs_lo = x_hi[:, bass.ds(c * CHUNK, CHUNK)], x_lo[:, bass.ds(c * CHUNK, CHUNK)]
                for kind, k in steps:
                    if kind == "pair_turn":
                        s, q = k // GPS, k % GPS
                        pe.wait_ge(built.sem, built.after(c, s))
                        pe.wait_ge(pair_kept.sem, pair_kept.after(c, k - 1))
                        for which in range(2):
                            for t in range(SEQ_TILES):
                                src = pairs_tm[:, t, which, q * QUAD:(q + 1) * QUAD, :]
                                at = which * SEQ + t * P
                                last = nc.tensor.transpose(TA[:, at:at + P], src.rearrange("p h w -> p (h w)"),
                                                           ident[:, :])
                        last.then_inc(pair_turned.sem, 1)
                    if kind == "score":
                        g, h = k // QUAD, k % QUAD
                        pe.wait_ge(pair_kept.sem, pair_kept.after(c, g))
                        pe.wait_ge(correlated.sem, correlated.after(c, k - 2))
                        rows = slice(h * SLOTS, h * SLOTS + TERMS)
                        keys, queries = pairs_T[g % 2][rows, 0, :], pairs_T[g % 2][rows, 1, :]
                        nc.tensor.matmul(S[k % 2][:, 0:SEQ], keys[:, 0:P], queries, start=True, stop=True)
                        nc.tensor.matmul(S[k % 2][:, SEQ:SEQ + P], keys[:, P:SEQ], queries[:, P:SEQ],
                                         start=True, stop=True).then_inc(scored.sem, 1)
                    if kind == "mix":
                        s, q = k // GPS, k % GPS
                        pe.wait_ge(mix_kept.sem, mix_kept.after(c, k - 1))
                        for power, src in enumerate((corr[k % 2], corr2[k % 2])):
                            if power == 0:
                                pe.wait_ge(correlated.sem, correlated.after(c, QUAD * k + QUAD - 1))
                            else:
                                pe.wait_ge(squared2.sem, squared2.after(c, QUAD * k + QUAD - 1))
                            for t in range(SEQ_TILES):
                                for h in range(QUAD):
                                    cols = slice(power * SEQ + t * P, power * SEQ + SEQ)
                                    rhs = src[:, h, 0:SEQ] if t == 0 else src[:, h, SEQ:SEQ + P]
                                    last = nc.tensor.matmul(U[h * SLOTS:(h + 1) * SLOTS, cols],
                                                            v32[s][:, t, q * QUAD + h, :], rhs,
                                                            start=(t == 0), stop=(t == 1), skip_group_check=True)
                        last.then_inc(mix_done.sem, 1)
                    if kind == "mix_turn":
                        pe.wait_ge(mix_kept.sem, mix_kept.after(c, k))
                        take_tb(kind, k)
                        for power in range(2):
                            for t in range(SEQ_TILES):
                                at = (power * SEQ_TILES + t) * P
                                last = nc.tensor.transpose(TB[:, at:at + P], mixed[:, power, t * P:(t + 1) * P], ident[:, :])
                        last.then_inc(tb_written.sem, 1)
                    if kind == "plain":
                        take_tb(kind, k)
                        W = HEADS * (HD + 1)
                        v9 = [v32[k][:, t, :, 0:HD + 1] for t in range(SEQ_TILES)]
                        nc.tensor.matmul(TB[:, 0:W], causal[:, :], v9[0], start=True, stop=True,
                                         skip_group_check=True)
                        nc.tensor.matmul(TB[:, W:2 * W], behind[:, :], v9[0], start=True, stop=False,
                                         skip_group_check=True)
                        nc.tensor.matmul(TB[:, W:2 * W], causal[:, :], v9[1], start=False, stop=True,
                                         skip_group_check=True).then_inc(tb_written.sem, 1)
                    if kind == "fit":
                        pe.wait_ge(fitted.sem, fitted.after(c, k))
                        take_tb(kind, k)
                        nc.tensor.matmul(TB[:, 0:HEADS], ones[:, :], inv[:, 0, :], start=True, stop=False)
                        nc.tensor.matmul(TB[:, 0:HEADS], ones[:, :], inv[:, 1, :], start=False,
                                         stop=True).then_inc(tb_written.sem, 1)
                    if kind == "attend":
                        pe.wait_ge(attended_ready.sem, attended_ready.after(c, k))
                        take_tb(kind, k)
                        for t in range(SEQ_TILES):
                            last = nc.tensor.transpose(TB[:, t * P:(t + 1) * P], attended[:, t, :], ident[:, :])
                        last.then_inc(tb_written.sem, 1)
                    if kind == "add_attended":
                        pe.wait_ge(tb_read.sem, tb_read.after(c, tb("attend", k)))
                        for t in range(SEQ_TILES):
                            last = nc.tensor.matmul(TB[:, t * D:(t + 1) * D], attended_T[:, t * P:(t + 1) * P],
                                                    wo[:, :], start=True, stop=True, skip_group_check=True)
                        last.then_inc(tb_written.sem, 1)
                    if kind == "up":
                        pe.wait_ge(silu_done.sem, silu_done.after(c, k - 1))
                        for which, (bank, done) in enumerate(((H1, up1_done), (H3, up3_done))):
                            if which == 1:
                                pe.wait_ge(glu_done.sem, glu_done.after(c, k - 1))
                            nc.tensor.matmul(bank[:, :], up_hi[:, k, which, :], xs_hi, start=True, stop=False)
                            nc.tensor.matmul(bank[:, :], up_hi[:, k, which, :], xs_lo, start=False, stop=False)
                            nc.tensor.matmul(bank[:, :], up_lo[:, k, which, :], xs_hi, start=False,
                                             stop=True).then_inc(done.sem, 1)
                    if kind == "down":
                        if k == 0:
                            pe.wait_ge(glu_done.sem, glu_done.after(c, 0))
                            pe.wait_ge(y_kept.sem, y_kept.after(c, -1))
                        else:
                            pe.wait_ge(gated_done.sem, gated_done.after(c, k - 1))
                        nc.tensor.matmul(Y[:, :], down_w[:, k, :], hidden[k % ACT_RING][:, :], start=(k == 0),
                                         stop=(k == PAIRS - 1)).then_inc(down_done.sem, 1)
                    if kind == "finish":
                        pe.wait_ge(y_kept.sem, y_kept.after(c, 0))
                        take_tb(kind, k)
                        for t in range(CHUNK_TILES):
                            last = nc.tensor.transpose(TB[:, t * P:(t + 1) * P], y_sb[:, t * P:(t + 1) * P],
                                                       ident[:, :])
                        last.then_inc(tb_written.sem, 1)


def kernel(L0_attn_x, L0_attn_Wg, L0_attn_bg, L0_attn_Wv, L0_attn_bv, L0_attn_Wo, L0_attn_bo, L0_ffn_Wg,
           L0_ffn_W1, L0_ffn_W2, L0_ffn_W3, L0_ffn_Ws1, L0_ffn_Ws2, L0_ffn_Ws3):
    import concourse.bacc as bacc
    from concourse.bass_utils import run_bass_kernel_spmd

    B, T, D = L0_attn_x.shape
    E, _, H = L0_ffn_W1.shape

    def tiles(a):
        return a.reshape(B * T // P, P, D).transpose(1, 0, 2)

    def up_pairs(shared, experts):
        return np.concatenate([shared[:, None, :], experts.transpose(1, 0, 2).reshape(D, E // 2, 2 * H)], axis=1)

    arrays = {
        "tokens_in": tiles(L0_attn_x),
        "project_in": np.concatenate([L0_attn_Wg.T, L0_attn_Wv.T, L0_ffn_Wg], axis=1),
        "bias_in": np.concatenate([L0_attn_bg, L0_attn_bv]),
        "out_bias_in": L0_attn_bo,
        "attn_out_in": L0_attn_Wo.T,
        "up_in": np.stack([up_pairs(L0_ffn_Ws1, L0_ffn_W1), up_pairs(L0_ffn_Ws3, L0_ffn_W3)], axis=2),
        "down_in": np.concatenate([L0_ffn_Ws2[:, None, :],
                                   L0_ffn_W2.reshape(E // 2, 2 * H, D).transpose(1, 0, 2)], axis=1),
    }
    arrays = {k: np.ascontiguousarray(a) for k, a in arrays.items()}
    nc = bacc.Bacc("TRN2", target_bir_lowering=False, num_devices=1)
    args = [nc.dram_tensor(k, a.shape, mybir.dt.from_np(a.dtype), kind="ExternalInput").ap()
            for k, a in arrays.items()]
    args.append(nc.dram_tensor("tokens_out", (P, B * T // P, D), mybir.dt.float32, kind="ExternalOutput").ap())
    windowed_attention_and_routed_experts(nc, *args)
    r = run_bass_kernel_spmd(nc, [arrays], core_ids=[0])
    return r.results[0]["tokens_out"].transpose(1, 0, 2).reshape(B, T, D)
```

```python
import numpy as np
import concourse.bass as bass
from concourse import mybir
from contextlib import ExitStack

P = 128


def windowed_attention_and_routed_experts(nc, tokens_in, project_in, bias_in, out_bias_in, attn_out_in,
                                          up_in, down_in, tokens_out):
    f32, f32r, bf16 = mybir.dt.float32, mybir.dt.float32r, mybir.dt.bfloat16
    ALU = mybir.AluOpType
    ACT = mybir.ActivationFunctionType
    AX = mybir.AxisListType

    TILES = tokens_in.shape[1]
    D = tokens_in.shape[2]
    HEADS, HD = 16, 8
    SEQ_TILES = 2
    BANDS = SEQ_TILES + 1
    EXPERTS = 32
    TOP = 4
    PAIRS = up_in.shape[1]
    CHUNK_TILES = 4
    CHUNK = CHUNK_TILES * P
    CHUNKS = TILES // CHUNK_TILES
    SEQS = CHUNK_TILES // SEQ_TILES
    QUAD = 4
    GROUPS = SEQS * HEADS // QUAD
    CHUNK_HEADS = GROUPS * QUAD
    GPS = GROUPS // SEQS
    SLOTS = 32
    TERMS = 3 * HD
    CAPACITY = 4 * (TILES * P * TOP) // EXPERTS
    SEQ = SEQ_TILES * P
    LN_EPS, CORR_EPS = 1e-5, 1e-8
    G_RING, L_RING, T_RING, ACT_RING = 4, 2, 4, 3
    PROJ = project_in.shape[1]
    GL = D + EXPERTS

    ctx = ExitStack()
    with ctx:
        def sb(name, shape, dt=f32):
            return ctx.enter_context(nc.sbuf_tensor(name, shape, dt))

        def pb(name):
            return ctx.enter_context(nc.psum_tensor(name, [P, 512], f32))

        def sem(name):
            return ctx.enter_context(nc.semaphore(name))

        class Count:

            def __init__(self, name, per):
                self.sem, self.per = sem(name), per

            def after(self, c, k):
                return c * self.per + (self.per + k + 1)

        x = sb("x", [P, TILES, D])
        xn = sb("xn", [P, TILES, D])
        xT = sb("xT", [P, TILES * P])
        x_hi = sb("x_hi", [P, TILES * P], f32r)
        x_lo = sb("x_lo", [P, TILES * P], f32r)
        up_hi = sb("up_hi", [P, PAIRS, 2, P], f32r)
        up_lo = sb("up_lo", [P, PAIRS, 2, P], f32r)
        UP_PIECES = 1 if PAIRS < 4 else 4
        up_bounds = [PAIRS * i // UP_PIECES for i in range(UP_PIECES + 1)]
        STAGE = max(b - a for a, b in zip(up_bounds, up_bounds[1:]))
        up_stage = sb("up_stage", [P, 2, STAGE, 2, P])
        down_w = sb("down_w", [P, PAIRS, D])
        proj_w = sb("proj_w", [P, PROJ])
        proj_b = sb("proj_b", [P, 2 * D])
        wo = sb("wo", [P, D])
        wo_b = sb("wo_b", [P, D])
        genes = sb("genes", [P, TILES, D])
        values = sb("values", [P, TILES, D])
        g_hi = sb("g_hi", [P, TILES, D], f32r)
        g_lo = sb("g_lo", [P, TILES, D])
        half_log = sb("half_log", [P, TILES, HEADS])
        gates = sb("gates", [P, TILES, EXPERTS])
        ident = sb("ident", [P, P])
        ones = sb("ones", [P, P])
        causal = sb("causal", [P, P])
        behind = sb("behind", [P, P])
        ones_b = sb("ones_b", [P, P], bf16)
        later_b = sb("later_b", [P, P], bf16)
        y_sb = sb("y_sb", [P, CHUNK])
        turned = y_sb
        turned_log = sb("turned_log", [P, 2 * P])

        pairs_tm = sb("pairs_tm", [P, 2, SEQ_TILES, HEADS, SLOTS])
        v32 = [sb(f"v32_{s}", [P, SEQ_TILES, HEADS, SLOTS]) for s in range(SEQS)]
        key_log = [sb(f"key_log{s}", [P, SEQ_TILES, HEADS]) for s in range(SEQS)]
        def room(buf, at, rows, cols):
            flat = buf[:, :, :].rearrange("p a b -> p (a b)")
            return flat[:, at * CHUNK:at * CHUNK + rows * cols].rearrange("p (a b) -> p a b", b=cols)

        pairs_T = [sb(f"pairs_T{i}", [P, 2, SEQ], f32r) for i in range(2)]
        row_log = [sb(f"row_log{i}", [P, SEQ_TILES, QUAD, P]) for i in range(L_RING)]
        damp = [sb(f"damp{i}", [P, BANDS, P]) for i in range(T_RING)]
        corr = [sb(f"corr{i}", [P, QUAD, BANDS * P]) for i in range(2)]
        corr2 = [sb("corr2_0", [P, QUAD, BANDS * P]), room(genes, 0, QUAD, BANDS * P)]
        mixed = room(xn, 0, 2, SEQ_TILES * P)
        sums = [sb(f"sums{s}", [P, 2, SEQ_TILES, HEADS, HD + 1]) for s in range(SEQS)]
        plain = [sb(f"plain{s}", [P, SEQ_TILES, HEADS, HD + 1]) for s in range(SEQS)]
        inv = sb("inv", [P, SEQ_TILES, HEADS])
        mean_d = sb("mean_d", [P, SEQ_TILES, HEADS])
        total = sb("total", [P, HEADS])
        alpha = sb("alpha", [P, SEQ_TILES, HEADS])
        num = sb("num", [P, SEQ_TILES, HEADS, HD + 1])
        num2 = sb("num2", [P, SEQ_TILES, HEADS, HD + 1])
        inv_sum = sb("inv_sum", [P, SEQ_TILES, HEADS])
        attended = sb("attended", [P, SEQ_TILES, D])
        attended_T = sb("attended_T", [P, SEQ])
        stage_flat = up_stage[:, :, :, :, :].rearrange("p i a b c -> p (i a b c)")
        gate_row = [stage_flat[:, i * CHUNK:(i + 1) * CHUNK] for i in range(G_RING)]
        silu = [xT[:, i * CHUNK:(i + 1) * CHUNK] for i in range(2)]
        glu = [xT[:, i * CHUNK:(i + 1) * CHUNK] for i in range(2, 4)]
        hidden = [room(xn, i + 1, 1, CHUNK)[:, 0, :] for i in range(ACT_RING)]

        stats = sb("stats", [P, TILES, 6])
        moments = sb("moments", [P, TILES, 2])
        var_eps = sb("var_eps", [P, TILES])
        std = sb("std", [P, TILES])
        rstd = sb("rstd", [P, TILES])
        newton = sb("newton", [P, TILES])
        norm2 = sb("norm2", [P, TILES, HEADS])
        norm = sb("norm", [P, TILES, HEADS])
        log_norm = sb("log_norm", [P, TILES, HEADS])
        logits = sb("logits", [P, TILES, EXPERTS])
        top8 = sb("top8", [P, TILES, 8])
        inv_norm = sb("inv_norm", [P, TILES, HEADS])
        per_tile = [sb(f"per_tile{i}", [P, TILES]) for i in range(3)]

        squares = xn
        unit = xn
        c_flat = corr[0][:, :, :].rearrange("p a b -> p (a b)")
        d_flat = corr2[0][:, :, :].rearrange("p a b -> p (a b)")
        e_flat = corr[1][:, :, :].rearrange("p a b -> p (a b)")
        f_flat = row_log[0][:, :, :, :].rearrange("p a b c -> p (a b c)")
        shifted_logits, prob, weight = (c_flat[:, i * 512:(i + 1) * 512].rearrange("p (t e) -> p t e", e=EXPERTS)
                                        for i in range(3))
        above, equal, ranked, chosen = (d_flat[:, i * 256:(i + 1) * 256].bitcast(bf16).rearrange(
            "p (t e) -> p t e", e=EXPERTS) for i in range(4))
        carried, place = (e_flat[:, i * 512:(i + 1) * 512].rearrange("p (e t) -> p e t", t=TILES) for i in range(2))
        kept = e_flat[:, 1024:1536].rearrange("p (e t) -> p e t", t=TILES)
        fresh_row = f_flat[:, 0:512].rearrange("p (t e) -> p t e", e=EXPERTS)
        fresh_expert = f_flat[:, 512:1024].rearrange("p (e t) -> p e t", t=TILES)

        H1, H3, Y, S0, S1, U, TA, TB = (pb(n) for n in ("H1", "H3", "Y", "S0", "S1", "U", "TA", "TB"))
        S = [S0, S1]

        gates_dram = nc.dram_tensor("gates_dram", (EXPERTS, TILES * P), f32, kind="Internal").ap()
        logs_dram = nc.dram_tensor("logs_dram", (TILES, HEADS, P), f32, kind="Internal").ap()

        steps = []

        def add(kind, k, n):
            if 0 <= k < n:
                steps.append((kind, k))

        HALF = CHUNK_HEADS // 2
        LAST = HALF + 6
        DENSE = 11
        pair_at = [[] for _ in range(LAST)]
        for p in range(1, PAIRS):
            pair_at[min(p * HALF // DENSE if p < DENSE else HALF + (p - DENSE), LAST - 1)].append(p)
        add("build", 0, SEQS)
        add("up", 0, PAIRS)
        add("pair_turn", 0, GROUPS)
        add("damp", 0, CHUNK_HEADS)
        add("damp", 1, CHUNK_HEADS)
        for t in range(LAST):
            for p in pair_at[t]:
                add("up", p, PAIRS)
                add("gate", p - 1, PAIRS)
            for s in range(SEQS):
                if t == (s + 1) * GPS * 2 + 2:
                    add("weigh", s, SEQS)
            if t % 2 == 0:
                add("pair_turn", t // 2 + 1, GROUPS)
            else:
                add("mix_turn", (t - 3) // 2, GROUPS)
            add("score", 2 * t, CHUNK_HEADS)
            add("damp", 2 * t + 2, CHUNK_HEADS)
            for p in pair_at[t]:
                add("down", p - 2, PAIRS)
            add("score", 2 * t + 1, CHUNK_HEADS)
            add("damp", 2 * t + 3, CHUNK_HEADS)
            if t % 2 == 0:
                add("mix", t // 2 - 1, GROUPS)
            for s in range(SEQS):
                end = (s + 1) * GPS * 2
                if s >= 1 and t == end - GPS * 2 - 4:
                    add("build", s, SEQS)
                if t == end - GPS * 2 + 3:
                    add("plain", s, SEQS)
                if t == end + 1:
                    add("fit", s, SEQS)
                if t == end + 4:
                    add("attend", s, SEQS)
                if t == end + 5:
                    add("add_attended", s, SEQS)
        add("gate", PAIRS - 1, PAIRS)
        add("down", PAIRS - 2, PAIRS)
        add("down", PAIRS - 1, PAIRS)
        add("finish", 0, 1)
        for kind, n in (("pair_turn", GROUPS), ("mix", GROUPS), ("mix_turn", GROUPS), ("score", CHUNK_HEADS),
                        ("damp", CHUNK_HEADS), ("up", PAIRS), ("down", PAIRS), ("fit", SEQS), ("weigh", SEQS),
                        ("plain", SEQS), ("attend", SEQS), ("add_attended", SEQS)):
            assert [k for what, k in steps if what == kind] == list(range(n)), kind

        tb_uses = [(kind, k) for kind, k in steps
                   if kind in ("mix_turn", "plain", "fit", "attend", "add_attended", "finish")]

        x_in = [sem(f"x_in{i}") for i in range(CHUNKS)]
        proj_in, consts_in, wo_in, down_ld = sem("proj_in"), sem("consts_in"), sem("wo_in"), sem("down_ld")
        up_ld = [sem(f"up_ld{i}") for i in range(2)]
        up_hi_done, up_lo_done = sem("up_hi_done"), sem("up_lo_done")
        made = sem("made")
        filled = sem("filled")
        v_step = sem("v_step")
        var_ready, std_ready = sem("var_ready"), sem("std_ready")
        rstd_ready, xn_even, xn_odd = sem("rstd_ready"), sem("xn_even"), sem("xn_odd")
        xT_turned, xT_kept, x_hi_kept, x_lo_kept = (sem(n) for n in ("xT_turned", "xT_kept", "x_hi_kept", "x_lo_kept"))
        projected, genes_kept, valued, values_kept = (sem(n) for n in (
            "projected", "genes_kept", "valued", "values_kept"))
        norm2_ready, norm_ready, clamped, logged = (sem(n) for n in (
            "norm2_ready", "norm_ready", "clamped", "logged"))
        unit_ready, g_hi_ready = sem("unit_ready"), sem("g_hi_ready")
        shifted, prob_ready, chosen_ready, counted, gates_ready = (sem(n) for n in (
            "shifted", "prob_ready", "chosen_ready", "counted", "gates_ready"))
        fourth_ready, kept_ready, inverted = sem("fourth_ready"), sem("kept_ready"), sem("inverted")
        half_ready, genes_ready = sem("half_ready"), sem("genes_ready")
        gates_turned, gates_kept, logs_turned, logs_kept = (sem(n) for n in (
            "gates_turned", "gates_kept", "logs_turned", "logs_kept"))
        gates_stored, logs_stored = sem("gates_stored"), sem("logs_stored")
        gate_ld = [sem(f"gate_ld{i}") for i in range(G_RING)]
        log_ld = [sem(f"log_ld{i}") for i in range(L_RING)]
        zeroed = sem("zeroed")
        stored, let_on = sem("stored"), sem("let_on")

        built = Count("built", SEQS)
        pair_turned, pair_kept = Count("pair_turned", GROUPS), Count("pair_kept", GROUPS)
        scored, damped = Count("scored", CHUNK_HEADS), Count("damped", CHUNK_HEADS)
        windowed, correlated = Count("windowed", CHUNK_HEADS), Count("correlated", CHUNK_HEADS)
        squared2 = Count("squared2", CHUNK_HEADS)
        mix_done, mix_kept = Count("mix_done", GROUPS), Count("mix_kept", GROUPS)
        tb_written, tb_read = Count("tb_written", len(tb_uses)), Count("tb_read", len(tb_uses))
        fitted, attended_ready = Count("fitted", SEQS), Count("attended_ready", SEQS)
        NORM_STEPS = 8
        norm_step = Count("norm_step", NORM_STEPS * SEQS)
        up1_done, up3_done = Count("up1_done", PAIRS), Count("up3_done", PAIRS)
        silu_done, glu_done = Count("silu_done", PAIRS), Count("glu_done", PAIRS)
        gated_done, down_done = Count("gated_done", PAIRS - 1), Count("down_done", PAIRS)
        biased = Count("biased", 1)
        y_kept, summed = Count("y_kept", 1), Count("summed", 1)

        def last_use(k, ring, per):
            return next(j for j in range(k - 1, k - 1 - per, -1) if (j % per) % ring == k % ring)

        def tb(kind, k):
            return tb_uses.index((kind, k))

        block = ctx.enter_context(nc.Block())

        @block.sync
        def _(sp):
            for c in range(CHUNKS):
                q = slice(c * CHUNK_TILES, (c + 1) * CHUNK_TILES)
                sp.dma_start(x[:, q, :], tokens_in[:, q, :]).then_inc(x_in[c], 16)
            sp.dma_start(proj_w[:, :], project_in).then_inc(proj_in, 16)
            sp.dma_start(proj_b[:, :], bias_in.partition_broadcast(P)).then_inc(consts_in, 16)
            sp.dma_start(wo_b[:, :], out_bias_in.partition_broadcast(P)).then_inc(consts_in, 16)
            for i in range(UP_PIECES):
                a, b = up_bounds[i], up_bounds[i + 1]
                if i >= 2:
                    sp.wait_ge(up_lo_done, i - 1)
                sp.dma_start(up_stage[:, i % 2, 0:b - a, :, :], up_in[:, a:b, :, :]).then_inc(up_ld[i % 2], 16)
            sp.dma_start(down_w[:, :, :], down_in).then_inc(down_ld, 16)
            sp.dma_start(wo[:, :], attn_out_in).then_inc(wo_in, 16)

            sp.wait_ge(logs_kept, 1)
            for i in range(2):
                rows = logs_dram.rearrange("t h p -> (t h) p")[i * P:(i + 1) * P, :]
                sp.dma_start(rows, turned_log[:, i * P:(i + 1) * P]).then_inc(logs_stored, 16)
            sp.wait_ge(gates_kept, 1)
            by_quarter = gates_dram.rearrange("e (c b p) -> b e c p", b=4, p=P)
            for b in range(4):
                sp.dma_start(by_quarter[b], turned[b * EXPERTS:(b + 1) * EXPERTS, :].rearrange(
                    "e (c p) -> e c p", p=P)).then_inc(gates_stored, 16)
            sp.wait_ge(logs_stored, 32)
            sp.wait_ge(gates_stored, 16 * 4)
            sp.wait_ge(up_lo_done, UP_PIECES)

            with sp.Fori(0, CHUNKS) as c:
                for kind, k in steps:
                    if kind == "damp" and k % QUAD == 0:
                        g = k // QUAD
                        s, q = g // GPS, g % GPS
                        sp.wait_ge(damped.sem, damped.after(c, QUAD * (g - L_RING) + QUAD - 1))
                        src = logs_dram[bass.ds(c * CHUNK_TILES + s * SEQ_TILES, SEQ_TILES),
                                        q * QUAD:(q + 1) * QUAD, :]
                        sp.dma_start(row_log[g % L_RING][:, :, :, :],
                                     src.partition_broadcast(P)).then_inc(log_ld[g % L_RING], 16)
                    if kind == "up" and k >= 1:
                        slot = (k - 1) % G_RING
                        sp.wait_ge(gated_done.sem, gated_done.after(c, k - 1 - G_RING))
                        for half in range(2):
                            row = gates_dram[2 * (k - 1) + half, bass.ds(c * CHUNK, CHUNK)]
                            sp.dma_start(gate_row[slot][half * 64:(half + 1) * 64, :],
                                         row.partition_broadcast(64)).then_inc(gate_ld[slot], 16)
                sp.wait_ge(summed.sem, summed.after(c, 0))
                sp.dma_start(tokens_out[:, bass.ds(c * CHUNK_TILES, CHUNK_TILES), :],
                             x[:, bass.ds(c * CHUNK_TILES, CHUNK_TILES), :]).then_inc(stored, 16)
            sp.wait_ge(stored, 16 * CHUNKS)

        @block.gpsimd
        def _(pool):
            n = [0]

            def chain(ins):
                n[0] += 1
                ins.then_inc(filled, 1)
                pool.wait_ge(filled, n[0])

            chain(nc.gpsimd.memset(ident[:, :], 0.0))
            nc.gpsimd.affine_select(out=ident[:, :], in_=ident[:, :], compare_op=ALU.not_equal, fill=1.0, base=0,
                                    pattern=[[-1, P]], channel_multiplier=1).then_inc(made, 1)
            chain(nc.gpsimd.memset(ones[:, :], 1.0))
            nc.gpsimd.affine_select(out=causal[:, :], in_=ones[:, :], compare_op=ALU.is_ge, fill=0.0, base=0,
                                    pattern=[[1, P]], channel_multiplier=-1).then_inc(made, 1)
            nc.gpsimd.affine_select(out=behind[:, :], in_=ones[:, :], compare_op=ALU.is_ge, fill=0.0, base=0,
                                    pattern=[[-1, P]], channel_multiplier=1).then_inc(made, 1)
            nc.gpsimd.memset(ones_b[:, :], 1.0).then_inc(made, 1)
            chain(nc.gpsimd.memset(later_b[:, :], 0.0))
            nc.gpsimd.affine_select(out=later_b[:, :], in_=later_b[:, :], compare_op=ALU.is_ge, fill=-1.0, base=0,
                                    pattern=[[1, P]], channel_multiplier=-1).then_inc(made, 1)
            nc.gpsimd.memset(fresh_row, 1.0).then_inc(filled, 1)
            nc.gpsimd.memset(fresh_expert, 1.0).then_inc(filled, 1)
            n[0] += 2
            pool.wait_ge(filled, n[0])
            nc.gpsimd.memset(fresh_row[:, :, 0:1], 0.0).then_inc(made, 1)
            nc.gpsimd.memset(fresh_expert[:, :, 0:1], 0.0).then_inc(made, 1)
            nc.gpsimd.memset(pairs_tm[:, :, :, :, :], 0.0).then_inc(filled, 1)
            n[0] += 1
            for s in range(SEQS):
                nc.gpsimd.memset(v32[s][:, :, :, :], 0.0).then_inc(filled, 1)
                n[0] += 1
            pool.wait_ge(filled, n[0])
            for s in range(SEQS):
                ins = nc.gpsimd.memset(v32[s][:, :, :, HD:HD + 1], 1.0)
                n[0] += 1
                ins.then_inc(filled, 1)
            pool.wait_ge(rstd_ready, 1)
            for t in range(1, TILES, 2):
                nc.gpsimd.tensor_scalar(xn[:, t, :], x[:, t, :], moments[:, t, 0:1], rstd[:, t:t + 1],
                                        ALU.subtract, ALU.mult).then_inc(xn_odd, 1)
            for i in range(max(CHUNKS, UP_PIECES)):
                if i < CHUNKS:
                    cols = slice(i * CHUNK, (i + 1) * CHUNK)
                    pool.wait_ge(x_hi_kept, i + 1)
                    nc.gpsimd.tensor_tensor(x_lo[:, cols], xT[:, cols], x_hi[:, cols].bitcast(f32),
                                            ALU.subtract).then_inc(x_lo_kept, 1)
                if i < UP_PIECES:
                    a, b = up_bounds[i], up_bounds[i + 1]
                    pool.wait_ge(up_hi_done, i + 1)
                    nc.gpsimd.tensor_tensor(up_lo[:, a:b, :, :], up_stage[:, i % 2, 0:b - a, :, :],
                                            up_hi[:, a:b, :, :].bitcast(f32), ALU.subtract).then_inc(up_lo_done, 1)
            for q in range(CHUNKS):
                r = slice(q * CHUNK_TILES, (q + 1) * CHUNK_TILES)
                pool.wait_ge(g_hi_ready, q + 1)
                nc.gpsimd.tensor_tensor(g_lo[:, r, :], unit[:, r, :], g_hi[:, r, :].bitcast(f32),
                                        ALU.subtract).then_inc(genes_ready, 1)

            pool.wait_ge(filled, n[0])
            pool.sem_inc(zeroed, 1)
            for count in (windowed, gated_done, biased):
                pool.sem_inc(count.sem, count.per)
            pool.wait_ge(consts_in, 32)
            pool.wait_ge(xn_even, TILES // 2)
            pool.wait_ge(xn_odd, TILES // 2)
            outside = pool.to_reg(-1.0)

            def go():
                pool.sem_inc(let_on, 1)

            with pool.Fori(0, CHUNKS) as c:
                for kind, k in steps:
                    if kind == "up" and k == 0:
                        r = bass.ds(c * CHUNK_TILES, CHUNK_TILES)
                        nc.gpsimd.tensor_tensor(x[:, r, :], x[:, r, :],
                                                wo_b[:, :].unsqueeze(1).to_broadcast([P, CHUNK_TILES, D]),
                                                ALU.add).then_inc(biased.sem, 1)
                    if kind == "damp":
                        pool.wait_ge(damped.sem, damped.after(c, k))
                        go()
                        t = damp[k % T_RING]
                        nc.gpsimd.affine_select(out=t[:, 0:3:2, :], in_=t[:, 0:3:2, :], compare_op=ALU.is_ge,
                                                fill=outside, base=0, pattern=[[0, 2], [1, P]], channel_multiplier=-1)
                        nc.gpsimd.affine_select(out=t[:, 1, :], in_=t[:, 1, :], compare_op=ALU.is_ge,
                                                fill=outside, base=0, pattern=[[-1, P]],
                                                channel_multiplier=1).then_inc(windowed.sem, 1)
                    if kind == "gate" and k >= 1:
                        slot = (k - 1) % G_RING
                        uses = (PAIRS - 1) // G_RING
                        pool.wait_ge(glu_done.sem, glu_done.after(c, k))
                        pool.wait_ge(gate_ld[slot], c * (32 * uses) + 32 * ((k - 1) // G_RING + 1))
                        pool.wait_ge(down_done.sem, down_done.after(c, last_use(k, ACT_RING, PAIRS)))
                        nc.gpsimd.tensor_tensor(hidden[k % ACT_RING][:, :], glu[k % 2][:, :],
                                                gate_row[slot][:, :], ALU.mult).then_inc(gated_done.sem, 1)

        @block.scalar
        def _(act):
            act.wait_ge(var_ready, 1)
            nc.scalar.activation(std[:, :], var_eps[:, :], ACT.Sqrt).then_inc(std_ready, 1)
            def keep_values(q):
                act.wait_ge(valued, q + 1)
                nc.scalar.activation(values[:, q * CHUNK_TILES:(q + 1) * CHUNK_TILES, :].rearrange("p t d -> p (t d)"),
                                     (Y, U)[q % 2][:, :], ACT.Copy).then_inc(values_kept, 1)

            def split_up(i):
                a, b = up_bounds[i], up_bounds[i + 1]
                act.wait_ge(up_ld[i % 2], 16 * (i // 2 + 1))
                nc.scalar.activation(up_hi[:, a:b, :, :], up_stage[:, i % 2, 0:b - a, :, :],
                                     ACT.Copy).then_inc(up_hi_done, 1)

            for q in range(CHUNKS):
                cols = slice(q * CHUNK, (q + 1) * CHUNK)
                act.wait_ge(xT_turned, q + 1)
                nc.scalar.activation(xT[:, cols], S[q % 2][:, :], ACT.Copy).then_inc(xT_kept, 1)
                nc.scalar.activation(x_hi[:, cols], S[q % 2][:, :], ACT.Copy).then_inc(x_hi_kept, 1)
                if q >= 1:
                    keep_values(q - 1)
                    if q - 1 < UP_PIECES:
                        split_up(q - 1)
            keep_values(CHUNKS - 1)
            act.wait_ge(norm2_ready, CHUNKS)
            nc.scalar.activation(norm[:, :, :], norm2[:, :, :], ACT.Sqrt).then_inc(norm_ready, 1)
            for i in range(CHUNKS - 1, UP_PIECES):
                split_up(i)
            act.wait_ge(shifted, 1)
            nc.scalar.activation(prob, shifted_logits, ACT.Exp).then_inc(prob_ready, 1)
            act.wait_ge(clamped, 1)
            nc.scalar.activation(log_norm[:, :, :], norm[:, :, :], ACT.Ln, scale=CORR_EPS ** -0.5).then_inc(logged, 1)
            act.wait_ge(logged, 1)
            nc.scalar.activation(half_log[:, :, :], log_norm[:, :, :], ACT.Copy, scale=0.5).then_inc(half_ready, 1)
            act.wait_ge(logs_turned, 1)
            nc.scalar.activation(turned_log[:, :], TB[:, 0:2 * P], ACT.Copy).then_inc(logs_kept, 1)
            act.wait_ge(gates_turned, 1)
            nc.scalar.activation(turned[:, :], TA[:, :], ACT.Copy).then_inc(gates_kept, 1)
            for q in range(CHUNKS):
                r = slice(q * CHUNK_TILES, (q + 1) * CHUNK_TILES)
                act.wait_ge(unit_ready, q + 1)
                nc.scalar.activation(g_hi[:, r, :], unit[:, r, :], ACT.Copy).then_inc(g_hi_ready, 1)

            for count in (damped, squared2, silu_done, y_kept):
                act.sem_inc(count.sem, count.per)
            with act.Fori(0, CHUNKS) as c:
                def square(k):
                    g, h = k // QUAD, k % QUAD
                    act.wait_ge(correlated.sem, correlated.after(c, k))
                    act.wait_ge(mix_done.sem, mix_done.after(c, g - 2))
                    nc.scalar.activation(corr2[g % 2][:, h, :], corr[g % 2][:, h, :], ACT.Square,
                                         scale=0.5).then_inc(squared2.sem, 1)

                for kind, k in steps:
                    if kind == "damp":
                        g, h = k // QUAD, k % QUAD
                        s = g // GPS
                        if h == 0:
                            act.wait_ge(log_ld[g % L_RING], c * (16 * GROUPS // L_RING) + 16 * (g // L_RING + 1))
                            act.wait_ge(built.sem, built.after(c, s))
                        act.wait_ge(correlated.sem, correlated.after(c, k - T_RING))
                        head = (g % GPS) * QUAD + h
                        rows = row_log[g % L_RING]
                        nc.scalar.activation(damp[k % T_RING][:, 0:2, :], rows[:, :, h, :], ACT.Tanh,
                                             bias=key_log[s][:, 0, head:head + 1])
                        nc.scalar.activation(damp[k % T_RING][:, 2, :], rows[:, 1, h, :], ACT.Tanh,
                                             bias=key_log[s][:, 1, head:head + 1]).then_inc(damped.sem, 1)
                    if kind == "score" and k >= 1:
                        square(k - 1)
                    if kind == "score" and k == CHUNK_HEADS - 1:
                        square(k)
                    if kind == "plain":
                        act.wait_ge(tb_written.sem, tb_written.after(c, tb("plain", k)))
                        act.wait_ge(norm_step.sem, norm_step.after(c, NORM_STEPS * (k + 1) - 1 - NORM_STEPS * SEQS))
                        nc.scalar.activation(plain[k][:, :, :, :].rearrange("p a b c -> p (a b c)"),
                                             TB[:, 0:SEQ_TILES * HEADS * (HD + 1)],
                                             ACT.Copy).then_inc(tb_read.sem, 1)
                    if kind == "up":
                        act.wait_ge(up1_done.sem, up1_done.after(c, k))
                        act.wait_ge(glu_done.sem, glu_done.after(c, last_use(k, 2, PAIRS)))
                        nc.scalar.activation(silu[k % 2][:, :], H1[:, :], ACT.Silu).then_inc(silu_done.sem, 1)
                    if kind == "attend":
                        act.wait_ge(tb_written.sem, tb_written.after(c, tb("attend", k)))
                        nc.scalar.activation(attended_T[:, :], TB[:, 0:SEQ], ACT.Copy).then_inc(tb_read.sem, 1)
                    if kind == "finish":
                        act.wait_ge(down_done.sem, down_done.after(c, PAIRS - 1))
                        act.wait_ge(tb_written.sem, tb_written.after(c, tb("finish", 0) - len(tb_uses)))
                        nc.scalar.activation(y_sb[:, :], Y[:, :], ACT.Copy).then_inc(y_kept.sem, 1)

        @block.vector
        def _(dve):
            n = [0]

            def chain(ins):
                n[0] += 1
                ins.then_inc(v_step, 1)
                dve.wait_ge(v_step, n[0])

            for q in range(CHUNKS):
                dve.wait_ge(x_in[q], 16)
                for t in range(q * CHUNK_TILES, (q + 1) * CHUNK_TILES):
                    last = nc.vector.bn_stats(stats[:, t, :], x[:, t, :])
            chain(last)
            for t in range(TILES):
                last = nc.vector.bn_aggr(moments[:, t, :], stats[:, t, :])
            chain(last)
            nc.vector.tensor_scalar(var_eps[:, :], moments[:, :, 1], LN_EPS, None, ALU.add).then_inc(var_ready, 1)
            dve.wait_ge(std_ready, 1)
            chain(nc.vector.reciprocal(rstd[:, :], std[:, :]))
            chain(nc.vector.tensor_tensor(newton[:, :], rstd[:, :], rstd[:, :], ALU.mult))
            dve.wait_ge(var_ready, 1)
            chain(nc.vector.tensor_tensor(newton[:, :], newton[:, :], var_eps[:, :], ALU.mult))
            chain(nc.vector.tensor_scalar(newton[:, :], newton[:, :], -0.5, 1.5, ALU.mult, ALU.add))
            nc.vector.tensor_tensor(rstd[:, :], rstd[:, :], newton[:, :], ALU.mult).then_inc(rstd_ready, 1)
            dve.wait_ge(rstd_ready, 1)
            for t in range(0, TILES, 2):
                nc.vector.tensor_scalar(xn[:, t, :], x[:, t, :], moments[:, t, 0:1], rstd[:, t:t + 1],
                                        ALU.subtract, ALU.mult).then_inc(xn_even, 1)
            dve.wait_ge(consts_in, 32)
            bias_b = proj_b[:, 0:D].unsqueeze(1).to_broadcast([P, 2, D])
            for q in range(CHUNKS):
                for i in range(q * CHUNK_TILES // 2, (q + 1) * CHUNK_TILES // 2):
                    dve.wait_ge(projected, i + 1)
                    both = (H1, H3)[i % 2][:, 0:2 * GL].rearrange("p (t w) -> p t w", w=GL)
                    nc.vector.tensor_copy(logits[:, 2 * i:2 * i + 2, :], both[:, :, D:GL])
                    last = nc.vector.tensor_tensor(genes[:, 2 * i:2 * i + 2, :], both[:, :, 0:D], bias_b, ALU.add)
                    last.then_inc(genes_kept, 1)
                dve.wait_ge(genes_kept, (q + 1) * CHUNK_TILES // 2)
                r = slice(q * CHUNK_TILES, (q + 1) * CHUNK_TILES)
                chain(nc.vector.tensor_tensor(squares[:, r, :], genes[:, r, :], genes[:, r, :], ALU.mult))
                nc.vector.tensor_reduce(norm2[:, r, :], squares[:, r, :].rearrange("p t (h d) -> p t h d", d=HD),
                                        AX.X, ALU.add).then_inc(norm2_ready, 1)

            for t in range(TILES):
                last = nc.vector.max(top8[:, t, :], logits[:, t, :])
            chain(last)
            chain(nc.vector.tensor_tensor(shifted_logits, logits[:, :, :],
                                          top8[:, :, 0:1].to_broadcast([P, TILES, EXPERTS]), ALU.subtract))
            nc.vector.tensor_tensor(per_tile[0][:, :], top8[:, :, TOP - 1], top8[:, :, 0],
                                    ALU.subtract).then_inc(fourth_ready, 1)
            nc.vector.tensor_scalar(shifted_logits, shifted_logits, -87.33, None, ALU.max).then_inc(shifted, 1)
            dve.wait_ge(fourth_ready, 1)
            chain(nc.vector.tensor_scalar(per_tile[0][:, :], per_tile[0][:, :], -87.33, None, ALU.max))
            dve.wait_ge(shifted, 1)
            dve.wait_ge(made, 7)
            fourth = per_tile[0][:, :].unsqueeze(2).to_broadcast([P, TILES, EXPERTS])
            chain(nc.vector.tensor_tensor(equal, shifted_logits, fourth, ALU.is_equal))
            nc.vector.tensor_tensor_scan(ranked.rearrange("p t e -> p (t e)"),
                                         fresh_row.rearrange("p t e -> p (t e)"),
                                         equal.rearrange("p t e -> p (t e)"), 0.0, ALU.mult, ALU.add)
            chain(nc.vector.tensor_tensor(above, shifted_logits, fourth, ALU.is_gt))
            chain(nc.vector.tensor_reduce(per_tile[1][:, :], above, AX.X, ALU.add))
            chain(nc.vector.tensor_scalar(per_tile[1][:, :], per_tile[1][:, :], -1.0, float(TOP), ALU.mult, ALU.add))
            left_b = per_tile[1][:, :].unsqueeze(2).to_broadcast([P, TILES, EXPERTS])
            chain(nc.vector.tensor_tensor(ranked, ranked, left_b, ALU.is_le))
            chain(nc.vector.tensor_tensor(equal, equal, ranked, ALU.mult))
            nc.vector.tensor_tensor(chosen, equal, above, ALU.add).then_inc(chosen_ready, 1)

            dve.wait_ge(norm_ready, 1)
            chain(nc.vector.tensor_scalar(norm2[:, :, :], norm[:, :, :], 1e-22, None, ALU.add))
            nc.vector.tensor_scalar(norm[:, :, :], norm[:, :, :], 1e-22, 1e14, ALU.max, ALU.min).then_inc(clamped, 1)
            nc.vector.reciprocal(inv_norm[:, :, :], norm2[:, :, :]).then_inc(inverted, 1)

            dve.wait_ge(counted, 1)
            chain(nc.vector.tensor_tensor_scan(carried.rearrange("p e t -> p (e t)"),
                                               fresh_expert.rearrange("p e t -> p (e t)"),
                                               S1[:, :], 0.0, ALU.mult, ALU.add))
            chain(nc.vector.tensor_tensor(place.rearrange("p e t -> p (e t)"), carried.rearrange("p e t -> p (e t)"),
                                          S0[:, :], ALU.add))
            nc.vector.scalar_tensor_tensor(out=kept, in0=place, scalar=float(CAPACITY),
                                           in1=chosen.rearrange("p t e -> p e t"), op0=ALU.is_le,
                                           op1=ALU.mult).then_inc(kept_ready, 1)
            dve.wait_ge(prob_ready, 1)
            chain(nc.vector.tensor_reduce(per_tile[0][:, :], prob, AX.X, ALU.add))
            chain(nc.vector.reciprocal(per_tile[2][:, :], per_tile[0][:, :]))
            share_b = per_tile[2][:, :].unsqueeze(2).to_broadcast([P, TILES, EXPERTS])
            chain(nc.vector.tensor_tensor(weight, prob, share_b, ALU.mult))
            dve.wait_ge(kept_ready, 1)
            nc.vector.tensor_tensor(gates[:, :, :], weight, kept.rearrange("p e t -> p t e"),
                                    ALU.mult).then_inc(gates_ready, 1)

            dve.wait_ge(inverted, 1)
            inv_b = inv_norm[:, :, :].unsqueeze(3).to_broadcast([P, TILES, HEADS, HD])
            for q in range(CHUNKS):
                r = slice(q * CHUNK_TILES, (q + 1) * CHUNK_TILES)
                chain(nc.vector.tensor_tensor(unit[:, r, :].rearrange("p t (h d) -> p t h d", d=HD),
                                              genes[:, r, :].rearrange("p t (h d) -> p t h d", d=HD),
                                              inv_b[:, r], ALU.mult))
                chain(nc.vector.tensor_scalar(g_lo[:, r, :], unit[:, r, :], 0.0, None, ALU.max))
                nc.vector.scalar_tensor_tensor(out=unit[:, r, :], in0=unit[:, r, :], scalar=0.0, in1=g_lo[:, r, :],
                                               op0=ALU.min, op1=ALU.add).then_inc(unit_ready, 1)

            for count in (built, pair_kept, mix_kept, correlated, glu_done, tb_read, fitted, attended_ready, norm_step, summed):
                dve.sem_inc(count.sem, count.per)
            dve.wait_ge(genes_ready, CHUNKS)
            dve.wait_ge(half_ready, 1)
            dve.wait_ge(values_kept, CHUNKS)
            dve.wait_ge(zeroed, 1)
            with dve.Fori(0, CHUNKS) as c:
                for kind, k in steps:
                    if kind == "build":
                        s = k
                        rows = bass.ds(c * CHUNK_TILES + s * SEQ_TILES, SEQ_TILES)
                        dve.wait_ge(pair_turned.sem, pair_turned.after(c, s * GPS - 1))
                        dve.wait_ge(mix_done.sem, mix_done.after(c, (s + 1) * GPS - 1 - GROUPS))
                        dve.wait_ge(damped.sem, damped.after(c, (s + 1) * GPS * QUAD - 1 - CHUNK_HEADS))

                        def heads(buf):
                            return buf.rearrange("p t (h d) -> p (t h) d", d=HD)

                        def part(which, at):
                            return pairs_tm[:, which].rearrange("p t h w -> p (t h) w")[:, :, at * HD:(at + 1) * HD]

                        def twice(which, step):
                            both = pairs_tm[:, which].rearrange("p t h (j d) -> p (t h) j d", d=HD)
                            return both[:, :, 0:step + 1:step, :]

                        hi, lo = heads(g_hi[:, rows, :].bitcast(f32)), heads(g_lo[:, rows, :])
                        hi2 = hi.unsqueeze(2).to_broadcast([P, SEQ_TILES * HEADS, 2, HD])
                        for dst, src in ((twice(0, 2), hi2), (part(0, 1), lo), (twice(1, 1), hi2), (part(1, 2), lo)):
                            nc.vector.tensor_copy(dst, src)
                        bias = proj_b[:, D:2 * D].rearrange("p (h d) -> p h d", d=HD)
                        nc.vector.tensor_tensor(v32[s][:, :, :, 0:HD],
                                                values[:, rows, :].rearrange("p t (h d) -> p t h d", d=HD),
                                                bias.unsqueeze(1).to_broadcast([P, SEQ_TILES, HEADS, HD]), ALU.add)
                        nc.vector.tensor_copy(key_log[s][:, :, :], half_log[:, rows, :]).then_inc(built.sem, 1)
                    if kind == "score":
                        g, h = k // QUAD, k % QUAD
                        dve.wait_ge(scored.sem, scored.after(c, k))
                        dve.wait_ge(windowed.sem, windowed.after(c, k))
                        dve.wait_ge(mix_done.sem, mix_done.after(c, g - 2))
                        nc.vector.scalar_tensor_tensor(
                            out=corr[g % 2][:, h, :], in0=damp[k % T_RING][:, :, :].rearrange("p a b -> p (a b)"),
                            scalar=1.0, in1=S[k % 2][:, 0:BANDS * P], op0=ALU.add,
                            op1=ALU.mult).then_inc(correlated.sem, 1)
                    if kind == "pair_turn":
                        dve.wait_ge(pair_turned.sem, pair_turned.after(c, k))
                        dve.wait_ge(scored.sem, scored.after(c, QUAD * (k - 2) + QUAD - 1))
                        nc.vector.tensor_copy(pairs_T[k % 2][:, :, :],
                                              TA[:, :].rearrange("p (w q) -> p w q", w=2)).then_inc(pair_kept.sem, 1)
                    if kind == "mix":
                        dve.wait_ge(mix_done.sem, mix_done.after(c, k))
                        dve.wait_ge(tb_written.sem, tb_written.after(
                            c, tb("mix_turn", k - 1) if k else tb("mix_turn", GROUPS - 1) - len(tb_uses)))
                        nc.vector.tensor_copy(mixed.rearrange("p a b -> p (a b)"), U[:, :]).then_inc(mix_kept.sem, 1)
                    if kind == "mix_turn":
                        dve.wait_ge(tb_written.sem, tb_written.after(c, tb("mix_turn", k)))
                        s, q = k // GPS, k % GPS
                        src = TB[:, :].rearrange("p (a h w) -> p a h w", h=QUAD, w=SLOTS)[:, :, :, 0:HD + 1]
                        dst = sums[s][:, :, :, q * QUAD:(q + 1) * QUAD, :].rearrange("p a b h w -> p (a b) h w")
                        nc.vector.tensor_copy(dst, src).then_inc(tb_read.sem, 1)
                    if kind == "up":
                        dve.wait_ge(up3_done.sem, up3_done.after(c, k))
                        dve.wait_ge(silu_done.sem, silu_done.after(c, k))
                        if k == 0:
                            dve.wait_ge(down_done.sem, down_done.after(c, last_use(k, ACT_RING, PAIRS)))
                            dst = hidden[0]
                        else:
                            dve.wait_ge(gated_done.sem, gated_done.after(c, k - 3))
                            dst = glu[k % 2]
                        nc.vector.tensor_tensor(dst[:, :], silu[k % 2][:, :], H3[:, :],
                                                ALU.mult).then_inc(glu_done.sem, 1)
                    first = NORM_STEPS * k

                    def own(j):
                        dve.wait_ge(norm_step.sem, norm_step.after(c, first + j))

                    if kind == "fit":
                        dve.wait_ge(tb_read.sem, tb_read.after(c, tb("mix_turn", (k + 1) * GPS - 1)))
                        nc.vector.tensor_scalar(mean_d[:, :, :], sums[k][:, 0, :, :, HD], 1.0 / (4 * SEQ), 1.0,
                                                ALU.mult, ALU.add).then_inc(norm_step.sem, 1)
                        own(0)
                        nc.vector.reciprocal(inv[:, :, :], mean_d[:, :, :]).then_inc(fitted.sem, 1)
                    if kind == "weigh":
                        dve.wait_ge(tb_written.sem, tb_written.after(c, tb("fit", k)))
                        nc.vector.reciprocal(total[:, :], TB[:, 0:HEADS]).then_inc(tb_read.sem, 1)
                        dve.wait_ge(tb_read.sem, tb_read.after(c, tb("fit", k)))
                        dve.wait_ge(fitted.sem, fitted.after(c, k))
                        nc.vector.scalar_tensor_tensor(
                            out=alpha[:, :, :], in0=inv[:, :, :], scalar=0.25,
                            in1=total[:, :].unsqueeze(1).to_broadcast([P, SEQ_TILES, HEADS]),
                            op0=ALU.mult, op1=ALU.mult).then_inc(norm_step.sem, 1)
                        own(1)
                        M = SEQ_TILES * HEADS
                        a_b = alpha[:, :, :].rearrange("p t h -> p (t h)").unsqueeze(2).to_broadcast([P, M, HD + 1])

                        def rows(buf):
                            return buf.rearrange("p t h w -> p (t h) w")

                        first_sum, second_sum = rows(sums[k][:, 0]), rows(sums[k][:, 1])
                        nc.vector.scalar_tensor_tensor(out=rows(num[:, :, :, :]), in0=second_sum, scalar=2.0, in1=a_b,
                                                       op0=ALU.mult, op1=ALU.mult).then_inc(norm_step.sem, 1)
                        own(2)
                        nc.vector.tensor_tensor(rows(num2[:, :, :, :]), rows(num[:, :, :, :]), first_sum,
                                                ALU.add).then_inc(norm_step.sem, 1)
                        own(3)
                        nc.vector.tensor_tensor(rows(num[:, :, :, :]), rows(num2[:, :, :, :]), a_b,
                                                ALU.mult).then_inc(norm_step.sem, 1)
                        own(4)
                        dve.wait_ge(tb_read.sem, tb_read.after(c, tb("plain", k)))
                        nc.vector.tensor_tensor(rows(num2[:, :, :, :]), rows(num[:, :, :, :]), rows(plain[k][:, :, :, :]),
                                                ALU.add).then_inc(norm_step.sem, 1)
                        own(5)
                        nc.vector.reciprocal(inv_sum[:, :, :], num2[:, :, :, HD]).then_inc(norm_step.sem, 1)
                        own(6)
                        dve.wait_ge(tb_written.sem, tb_written.after(
                            c, tb("attend", k - 1) if k else tb("attend", SEQS - 1) - len(tb_uses)))
                        nc.vector.tensor_tensor(
                            attended[:, :, :].rearrange("p t (h w) -> p (t h) w", w=HD),
                            rows(num2[:, :, :, 0:HD]),
                            inv_sum[:, :, :].rearrange("p t h -> p (t h)").unsqueeze(2).to_broadcast([P, M, HD]),
                            ALU.mult).then_inc(attended_ready.sem, 1)
                        dve.wait_ge(attended_ready.sem, attended_ready.after(c, k))
                        dve.sem_inc(norm_step.sem, 1)
                    if kind == "add_attended":
                        dve.wait_ge(tb_written.sem, tb_written.after(c, tb("add_attended", k)))
                        dve.wait_ge(biased.sem, biased.after(c, 0))
                        r = bass.ds(c * CHUNK_TILES + k * SEQ_TILES, SEQ_TILES)
                        nc.vector.tensor_tensor(x[:, r, :], TB[:, 0:SEQ_TILES * D].rearrange("p (t d) -> p t d", d=D),
                                                x[:, r, :], ALU.add).then_inc(tb_read.sem, 1)
                    if kind == "finish":
                        dve.wait_ge(tb_written.sem, tb_written.after(c, tb("finish", 0)))
                        dve.wait_ge(tb_read.sem, tb_read.after(c, tb("add_attended", SEQS - 1)))
                        r = bass.ds(c * CHUNK_TILES, CHUNK_TILES)
                        nc.vector.tensor_tensor(x[:, r, :], TB[:, :].rearrange("p (t d) -> p t d", d=D),
                                                x[:, r, :], ALU.add).then_inc(summed.sem, 1)
                        dve.wait_ge(summed.sem, summed.after(c, 0))
                        dve.sem_inc(tb_read.sem, 1)

        @block.tensor
        def _(pe):
            pe.wait_ge(made, 7)
            pe.wait_ge(proj_in, 16)

            def turn_tokens(q):
                if q >= 2:
                    pe.wait_ge(x_hi_kept, q - 1)
                pe.wait_ge(xn_even, (q + 1) * CHUNK_TILES // 2)
                pe.wait_ge(xn_odd, (q + 1) * CHUNK_TILES // 2)
                for j in range(CHUNK_TILES):
                    last = nc.tensor.transpose(S[q % 2][:, j * P:(j + 1) * P], xn[:, q * CHUNK_TILES + j, :],
                                               ident[:, :])
                last.then_inc(xT_turned, 1)

            turn_tokens(0)
            for q in range(CHUNKS):
                if q + 1 < CHUNKS:
                    turn_tokens(q + 1)
                pe.wait_ge(xT_kept, q + 1)
                for i in range(q * CHUNK_TILES // 2, (q + 1) * CHUNK_TILES // 2):
                    if i >= 2:
                        pe.wait_ge(genes_kept, i - 1)
                    for j in range(2):
                        t = 2 * i + j
                        last = nc.tensor.matmul((H1, H3)[i % 2][:, j * GL:(j + 1) * GL], xT[:, t * P:(t + 1) * P],
                                                proj_w[:, 0:GL], start=True, stop=True, skip_group_check=True)
                    last.then_inc(projected, 1)
                if q >= 2:
                    pe.wait_ge(values_kept, q - 1)
                for j in range(CHUNK_TILES):
                    t = q * CHUNK_TILES + j
                    last = nc.tensor.matmul((Y, U)[q % 2][:, j * P:(j + 1) * P], xT[:, t * P:(t + 1) * P],
                                            proj_w[:, GL:PROJ], start=True, stop=True, skip_group_check=True)
                last.then_inc(valued, 1)
            pe.wait_ge(chosen_ready, 1)
            pe.wait_ge(x_hi_kept, CHUNKS)
            flat = chosen.rearrange("p t e -> p e t")
            nc.tensor.matmul(S0[:, :], later_b[:, :], flat, start=True, stop=True)
            nc.tensor.matmul(S1[:, :], ones_b[:, :], flat, start=True, stop=True).then_inc(counted, 1)
            pe.wait_ge(half_ready, 1)
            for i in range(2):
                last = nc.tensor.transpose(TB[:, i * P:(i + 1) * P],
                                           half_log[:, 8 * i:8 * (i + 1), :].rearrange("p t h -> p (t h)"),
                                           ident[:, :])
            last.then_inc(logs_turned, 1)
            pe.wait_ge(gates_ready, 1)
            for i in range(4):
                last = nc.tensor.transpose(TA[:, i * P:(i + 1) * P],
                                           gates[:, 4 * i:4 * (i + 1), :].rearrange("p t e -> p (t e)"), ident[:, :])
            last.then_inc(gates_turned, 1)
            pe.wait_ge(gates_kept, 1)
            pe.wait_ge(logs_kept, 1)
            pe.wait_ge(up_lo_done, UP_PIECES)
            pe.wait_ge(x_lo_kept, CHUNKS)
            pe.wait_ge(values_kept, CHUNKS)
            pe.wait_ge(down_ld, 16)
            pe.wait_ge(wo_in, 16)

            for count in (pair_turned, scored, mix_done, tb_written, up1_done, up3_done, down_done):
                pe.sem_inc(count.sem, count.per)
            with pe.Fori(0, CHUNKS) as c:
                def take_tb(kind, k):
                    pe.wait_ge(tb_read.sem, tb_read.after(c, tb(kind, k) - 1))

                xs_hi, xs_lo = x_hi[:, bass.ds(c * CHUNK, CHUNK)], x_lo[:, bass.ds(c * CHUNK, CHUNK)]
                for kind, k in steps:
                    if kind == "pair_turn":
                        s, q = k // GPS, k % GPS
                        pe.wait_ge(built.sem, built.after(c, s))
                        pe.wait_ge(pair_kept.sem, pair_kept.after(c, k - 1))
                        for which in range(2):
                            for t in range(SEQ_TILES):
                                src = pairs_tm[:, which, t, q * QUAD:(q + 1) * QUAD, :]
                                at = which * SEQ + t * P
                                last = nc.tensor.transpose(TA[:, at:at + P], src.rearrange("p h w -> p (h w)"),
                                                           ident[:, :])
                        last.then_inc(pair_turned.sem, 1)
                    if kind == "score":
                        g, h = k // QUAD, k % QUAD
                        pe.wait_ge(pair_kept.sem, pair_kept.after(c, g))
                        pe.wait_ge(correlated.sem, correlated.after(c, k - 2))
                        rows = slice(h * SLOTS, h * SLOTS + TERMS)
                        keys, queries = pairs_T[g % 2][rows, 0, :], pairs_T[g % 2][rows, 1, :]
                        nc.tensor.matmul(S[k % 2][:, 0:SEQ], keys[:, 0:P], queries, start=True, stop=True)
                        nc.tensor.matmul(S[k % 2][:, SEQ:SEQ + P], keys[:, P:SEQ], queries[:, P:SEQ],
                                         start=True, stop=True).then_inc(scored.sem, 1)
                    if kind == "mix":
                        s, q = k // GPS, k % GPS
                        pe.wait_ge(mix_kept.sem, mix_kept.after(c, k - 1))
                        for power, src in enumerate((corr[k % 2], corr2[k % 2])):
                            if power == 0:
                                pe.wait_ge(correlated.sem, correlated.after(c, QUAD * k + QUAD - 1))
                            else:
                                pe.wait_ge(squared2.sem, squared2.after(c, QUAD * k + QUAD - 1))
                            for t in range(SEQ_TILES):
                                for h in range(QUAD):
                                    cols = slice(power * SEQ + t * P, power * SEQ + SEQ)
                                    rhs = src[:, h, 0:SEQ] if t == 0 else src[:, h, SEQ:SEQ + P]
                                    last = nc.tensor.matmul(U[h * SLOTS:(h + 1) * SLOTS, cols],
                                                            v32[s][:, t, q * QUAD + h, :], rhs,
                                                            start=(t == 0), stop=(t == 1), skip_group_check=True)
                        last.then_inc(mix_done.sem, 1)
                    if kind == "mix_turn":
                        pe.wait_ge(mix_kept.sem, mix_kept.after(c, k))
                        take_tb(kind, k)
                        for power in range(2):
                            for t in range(SEQ_TILES):
                                at = (power * SEQ_TILES + t) * P
                                last = nc.tensor.transpose(TB[:, at:at + P], mixed[:, power, t * P:(t + 1) * P], ident[:, :])
                        last.then_inc(tb_written.sem, 1)
                    if kind == "plain":
                        take_tb(kind, k)
                        W = HEADS * (HD + 1)
                        v9 = [v32[k][:, t, :, 0:HD + 1] for t in range(SEQ_TILES)]
                        nc.tensor.matmul(TB[:, 0:W], causal[:, :], v9[0], start=True, stop=True,
                                         skip_group_check=True)
                        nc.tensor.matmul(TB[:, W:2 * W], behind[:, :], v9[0], start=True, stop=False,
                                         skip_group_check=True)
                        nc.tensor.matmul(TB[:, W:2 * W], causal[:, :], v9[1], start=False, stop=True,
                                         skip_group_check=True).then_inc(tb_written.sem, 1)
                    if kind == "fit":
                        pe.wait_ge(fitted.sem, fitted.after(c, k))
                        take_tb(kind, k)
                        nc.tensor.matmul(TB[:, 0:HEADS], ones[:, :], inv[:, 0, :], start=True, stop=False)
                        nc.tensor.matmul(TB[:, 0:HEADS], ones[:, :], inv[:, 1, :], start=False,
                                         stop=True).then_inc(tb_written.sem, 1)
                    if kind == "attend":
                        pe.wait_ge(attended_ready.sem, attended_ready.after(c, k))
                        take_tb(kind, k)
                        for t in range(SEQ_TILES):
                            last = nc.tensor.transpose(TB[:, t * P:(t + 1) * P], attended[:, t, :], ident[:, :])
                        last.then_inc(tb_written.sem, 1)
                    if kind == "add_attended":
                        pe.wait_ge(tb_read.sem, tb_read.after(c, tb("attend", k)))
                        take_tb(kind, k)
                        for t in range(SEQ_TILES):
                            last = nc.tensor.matmul(TB[:, t * D:(t + 1) * D], attended_T[:, t * P:(t + 1) * P],
                                                    wo[:, :], start=True, stop=True, skip_group_check=True)
                        last.then_inc(tb_written.sem, 1)
                    if kind == "up":
                        pe.wait_ge(silu_done.sem, silu_done.after(c, k - 1))
                        for which, (bank, done) in enumerate(((H1, up1_done), (H3, up3_done))):
                            if which == 1:
                                pe.wait_ge(glu_done.sem, glu_done.after(c, k - 1))
                            nc.tensor.matmul(bank[:, :], up_hi[:, k, which, :], xs_hi, start=True, stop=False)
                            nc.tensor.matmul(bank[:, :], up_hi[:, k, which, :], xs_lo, start=False, stop=False)
                            nc.tensor.matmul(bank[:, :], up_lo[:, k, which, :], xs_hi, start=False,
                                             stop=True).then_inc(done.sem, 1)
                    if kind == "down":
                        if k == 0:
                            pe.wait_ge(glu_done.sem, glu_done.after(c, 0))
                            pe.wait_ge(y_kept.sem, y_kept.after(c, -1))
                        else:
                            pe.wait_ge(gated_done.sem, gated_done.after(c, k - 1))
                        nc.tensor.matmul(Y[:, :], down_w[:, k, :], hidden[k % ACT_RING][:, :], start=(k == 0),
                                         stop=(k == PAIRS - 1)).then_inc(down_done.sem, 1)
                    if kind == "finish":
                        pe.wait_ge(y_kept.sem, y_kept.after(c, 0))
                        take_tb(kind, k)
                        for t in range(CHUNK_TILES):
                            last = nc.tensor.transpose(TB[:, t * P:(t + 1) * P], y_sb[:, t * P:(t + 1) * P],
                                                       ident[:, :])
                        last.then_inc(tb_written.sem, 1)


def kernel(L0_attn_x, L0_attn_Wg, L0_attn_bg, L0_attn_Wv, L0_attn_bv, L0_attn_Wo, L0_attn_bo, L0_ffn_Wg,
           L0_ffn_W1, L0_ffn_W2, L0_ffn_W3, L0_ffn_Ws1, L0_ffn_Ws2, L0_ffn_Ws3):
    import concourse.bacc as bacc
    from concourse.bass_utils import run_bass_kernel_spmd

    B, T, D = L0_attn_x.shape
    E, _, H = L0_ffn_W1.shape

    def tiles(a):
        return a.reshape(B * T // P, P, D).transpose(1, 0, 2)

    def up_pairs(shared, experts):
        return np.concatenate([shared[:, None, :], experts.transpose(1, 0, 2).reshape(D, E // 2, 2 * H)], axis=1)

    arrays = {
        "tokens_in": tiles(L0_attn_x),
        "project_in": np.concatenate([L0_attn_Wg.T, L0_ffn_Wg, L0_attn_Wv.T], axis=1),
        "bias_in": np.concatenate([L0_attn_bg, L0_attn_bv]),
        "out_bias_in": L0_attn_bo,
        "attn_out_in": L0_attn_Wo.T,
        "up_in": np.stack([up_pairs(L0_ffn_Ws1, L0_ffn_W1), up_pairs(L0_ffn_Ws3, L0_ffn_W3)], axis=2),
        "down_in": np.concatenate([L0_ffn_Ws2[:, None, :],
                                   L0_ffn_W2.reshape(E // 2, 2 * H, D).transpose(1, 0, 2)], axis=1),
    }
    arrays = {k: np.ascontiguousarray(a) for k, a in arrays.items()}
    nc = bacc.Bacc("TRN2", target_bir_lowering=False, num_devices=1)
    args = [nc.dram_tensor(k, a.shape, mybir.dt.from_np(a.dtype), kind="ExternalInput").ap()
            for k, a in arrays.items()]
    args.append(nc.dram_tensor("tokens_out", (P, B * T // P, D), mybir.dt.float32, kind="ExternalOutput").ap())
    windowed_attention_and_routed_experts(nc, *args)
    r = run_bass_kernel_spmd(nc, [arrays], core_ids=[0])
    return r.results[0]["tokens_out"].transpose(1, 0, 2).reshape(B, T, D)
```

```python
import numpy as np
import concourse.bass as bass
from concourse import mybir
from contextlib import ExitStack

P = 128


def windowed_attention_and_routed_experts(nc, tokens_in, project_in, bias_in, out_bias_in, attn_out_in,
                                          up_in, down_in, tokens_out):
    f32, f32r, bf16 = mybir.dt.float32, mybir.dt.float32r, mybir.dt.bfloat16
    ALU = mybir.AluOpType
    ACT = mybir.ActivationFunctionType
    AX = mybir.AxisListType

    TILES = tokens_in.shape[1]
    D = tokens_in.shape[2]
    HEADS, HD = 16, 8
    SEQ_TILES = 2
    BANDS = SEQ_TILES + 1
    EXPERTS = 32
    TOP = 4
    PAIRS = up_in.shape[1]
    CHUNK_TILES = 4
    CHUNK = CHUNK_TILES * P
    CHUNKS = TILES // CHUNK_TILES
    SEQS = CHUNK_TILES // SEQ_TILES
    QUAD = 4
    GROUPS = SEQS * HEADS // QUAD
    CHUNK_HEADS = GROUPS * QUAD
    GPS = GROUPS // SEQS
    SLOTS = 32
    TERMS = 3 * HD
    CAPACITY = 4 * (TILES * P * TOP) // EXPERTS
    SEQ = SEQ_TILES * P
    LN_EPS, CORR_EPS = 1e-5, 1e-8
    G_RING, L_RING, T_RING = 4, 2, 4
    PROJ = project_in.shape[1]
    GL = D + EXPERTS

    ctx = ExitStack()
    with ctx:
        def sb(name, shape, dt=f32):
            return ctx.enter_context(nc.sbuf_tensor(name, shape, dt))

        def pb(name):
            return ctx.enter_context(nc.psum_tensor(name, [P, 512], f32))

        def sem(name):
            return ctx.enter_context(nc.semaphore(name))

        class Count:

            def __init__(self, name, per):
                self.sem, self.per = sem(name), per

            def after(self, c, k):
                return c * self.per + (self.per + k + 1)

        x = sb("x", [P, TILES, D])
        xT = sb("xT", [P, TILES * P])
        x_hi = sb("x_hi", [P, TILES * P], f32r)
        x_lo = sb("x_lo", [P, TILES * P], f32r)
        up_hi = sb("up_hi", [P, PAIRS, 2, P], f32r)
        up_lo = sb("up_lo", [P, PAIRS, 2, P], f32r)
        STAGE = 1280
        up_stage = sb("up_stage", [P, 2, STAGE])
        down_hi = sb("down_hi", [P, PAIRS, D], f32r)
        down_lo = sb("down_lo", [P, PAIRS, D], f32r)

        def cut(high, low, source, bounds):
            for a, b in zip(bounds, bounds[1:]):
                yield tuple(buf[:, a:b].rearrange("p a b c -> p (a b c)" if len(buf.shape) == 4 else "p a b -> p (a b)")
                            for buf in (high, low, source))

        pieces = [*cut(up_hi, up_lo, up_in, [PAIRS * i // 4 for i in range(5)]),
                  *cut(down_hi, down_lo, down_in, [0, PAIRS // 2, PAIRS])]
        proj_b = sb("proj_b", [P, 2 * D])
        wo = sb("wo", [P, D])
        wo_b = sb("wo_b", [P, D])
        values = sb("values", [P, TILES, D])
        g_hi = sb("g_hi", [P, TILES, D], f32r)
        g_lo = sb("g_lo", [P, TILES, D])
        half_log = sb("half_log", [P, TILES, HEADS])
        outcome = sb("outcome", [P, 2, SEQ_TILES * D])
        gates = outcome[:, :, :].rearrange("p a (t e) -> p (a t) e", e=EXPERTS)
        ident = sb("ident", [P, P])
        ones = sb("ones", [P, P])
        causal = sb("causal", [P, P])
        behind = sb("behind", [P, P])
        ones_b = sb("ones_b", [P, P], bf16)
        later_b = sb("later_b", [P, P], bf16)
        y_sb = sb("y_sb", [P, CHUNK])
        turned = y_sb

        pairs_tm = sb("pairs_tm", [P, 2, SEQ_TILES, HEADS, SLOTS])
        v32 = [sb(f"v32_{s}", [P, SEQ_TILES, HEADS, SLOTS]) for s in range(SEQS)]
        key_log = [sb(f"key_log{s}", [P, SEQ_TILES, HEADS]) for s in range(SEQS)]
        pairs_T = [sb(f"pairs_T{i}", [P, 2, SEQ], f32r) for i in range(2)]
        row_log = [sb(f"row_log{i}", [P, SEQ_TILES, QUAD, P]) for i in range(L_RING)]
        damp = [sb(f"damp{i}", [P, BANDS, P]) for i in range(T_RING)]
        corr = [sb(f"corr{i}", [P, QUAD, BANDS * P]) for i in range(2)]
        corr2_first = sb("corr2_0", [P, QUAD, BANDS * P])
        sums = [sb(f"sums{s}", [P, 2, SEQ_TILES, HEADS, HD + 1]) for s in range(SEQS)]
        plain = [sb(f"plain{s}", [P, SEQ_TILES, HEADS, HD + 1]) for s in range(SEQS)]
        inv = sb("inv", [P, SEQ_TILES, HEADS])
        mean_d = sb("mean_d", [P, SEQ_TILES, HEADS])
        total = sb("total", [P, HEADS])
        alpha = sb("alpha", [P, SEQ_TILES, HEADS])
        num = sb("num", [P, SEQ_TILES, HEADS, HD + 1])
        num2 = sb("num2", [P, SEQ_TILES, HEADS, HD + 1])
        inv_sum = sb("inv_sum", [P, SEQ_TILES, HEADS])
        attended = outcome[:, 0, :].rearrange("p (t d) -> p t d", d=D)
        attended_T = outcome[:, 1, :]
        stage_flat = up_stage[:, :, :].rearrange("p i a -> p (i a)")
        gate_row = [stage_flat[:, i * CHUNK:(i + 1) * CHUNK] for i in range(G_RING)]
        silu = xT[:, 0:CHUNK]
        hidden = [xT[:, (i + 1) * CHUNK:(i + 2) * CHUNK] for i in range(3)]
        hidden_slot = [k % 3 for k in range(PAIRS)]

        def early(buf, rows, cols, at=0):
            flat = buf[:].rearrange({4: "p a b c -> p (a b c)", 5: "p a b c d -> p (a b c d)"}[len(buf.shape)])
            return flat[:, at:at + rows * cols].rearrange("p (a b) -> p a b", b=cols)

        turned_log = early(plain[1], 1, 2 * P)[:, 0, :]
        proj_w = damp[T_RING - 1][:, :, :].rearrange("p a b -> p (a b)")[:, 0:PROJ]
        stats = early(sums[1], TILES, 6, at=TILES * (HEADS + 8))
        fresh_expert = early(sums[0], EXPERTS, TILES)
        moments = sb("moments", [P, TILES, 2])
        var_eps = sb("var_eps", [P, TILES])
        std = sb("std", [P, TILES])
        rstd = sb("rstd", [P, TILES])
        newton = sb("newton", [P, TILES])
        norm2 = early(num, TILES, HEADS)
        norm = early(num2, TILES, HEADS)
        top8 = early(sums[1], TILES, 8, at=TILES * HEADS)
        inv_norm = early(sums[1], TILES, HEADS)
        per_tile = [sb(f"per_tile{i}", [P, TILES]) for i in range(3)]

        with ExitStack() as early_ctx:
            xn, genes, logits = (early_ctx.enter_context(nc.sbuf_tensor(name, [P, TILES, w], f32))
                                 for name, w in (("xn", D), ("genes", D), ("logits", EXPERTS)))
        hidden_lo = [sb(f"hidden_lo{i}", [P, CHUNK], f32r) for i in range(3)]
        hidden_hi = [sb(f"hidden_hi{i}", [P, CHUNK], f32r) for i in range(3)]
        mixed = stage_flat[:, G_RING * CHUNK:(G_RING + 1) * CHUNK].rearrange("p (a b) -> p a b", a=2)
        corr2 = [corr2_first, sb("corr2_1", [P, QUAD, BANDS * P])]

        squares = xn
        unit = xn
        c_flat = corr[0][:, :, :].rearrange("p a b -> p (a b)")
        d_flat = corr2[0][:, :, :].rearrange("p a b -> p (a b)")
        e_flat = corr[1][:, :, :].rearrange("p a b -> p (a b)")
        f_flat = row_log[0][:, :, :, :].rearrange("p a b c -> p (a b c)")
        shifted_logits, prob, weight = (c_flat[:, i * 512:(i + 1) * 512].rearrange("p (t e) -> p t e", e=EXPERTS)
                                        for i in range(3))
        above, equal, ranked, chosen = (d_flat[:, i * 256:(i + 1) * 256].bitcast(bf16).rearrange(
            "p (t e) -> p t e", e=EXPERTS) for i in range(4))
        carried, place = (e_flat[:, i * 512:(i + 1) * 512].rearrange("p (e t) -> p e t", t=TILES) for i in range(2))
        kept = e_flat[:, 1024:1536].rearrange("p (e t) -> p e t", t=TILES)
        fresh_row = f_flat[:, 0:512].rearrange("p (t e) -> p t e", e=EXPERTS)

        H1, H3, Y, S0, S1, U, TA, TB = (pb(n) for n in ("H1", "H3", "Y", "S0", "S1", "U", "TA", "TB"))
        S = [S0, S1]

        gates_dram = nc.dram_tensor("gates_dram", (EXPERTS, TILES * P), f32, kind="Internal").ap()
        logs_dram = nc.dram_tensor("logs_dram", (TILES, HEADS, P), f32, kind="Internal").ap()

        TURN = CHUNK_HEADS // 2
        SLOTS_AHEAD = 7
        first_time = {
            "pair_turn": (0.09, GROUPS),
            "score": (0.95, CHUNK_HEADS),
            "mix_corr": (3.48, GROUPS),
            "mix_square": (3.59, GROUPS),
            "mix_turn": (4.44, GROUPS),
            "up1": (2.24, PAIRS),
            "up3": (2.60, PAIRS),
            "down": (6.23, PAIRS),
            "plain": (1.38, SEQS),
            "fit": (11.11, SEQS),
            "attend": (12.22, SEQS),
            "add_attended": (12.31, SEQS),
            "finish": (20.99, 1),
            "damp": (0.57, CHUNK_HEADS),
            "square": (2.39, CHUNK_HEADS),
            "silu": (3.29, PAIRS),
            "high": (5.22, PAIRS),
            "plain_keep": (2.47, SEQS),
            "attend_keep": (12.58, SEQS),
            "y_keep": (21.12, 1),
            "build": (1.11, SEQS),
            "pair_keep": (2.09, GROUPS),
            "correlate": (2.91, CHUNK_HEADS),
            "mix_keep": (5.54, GROUPS),
            "sum_keep": (6.37, GROUPS),
            "glu": (4.64, PAIRS),
            "low": (6.62, PAIRS),
            "denominator": (12.44, SEQS),
            "weigh": (13.36, SEQS),
            "add_keep": (13.79, SEQS),
            "finish_keep": (22.44, 1),
            "window": (0.60, CHUNK_HEADS),
            "gate": (3.54, PAIRS),
            "bias": (3.28, 1),
            "log_rows": (-3.67, GROUPS),
            "gate_rows": (0.25, PAIRS),
            "store": (19.78, 1),
        }
        pair_kinds = ("up1", "up3", "silu", "glu", "gate", "high", "low", "down", "gate_rows")
        timed = []
        for kind, (first, count) in first_time.items():
            spacing = TURN / count * (0.93 if kind in pair_kinds else 1)
            for k in range(count):
                at = first + k * spacing
                if kind == "build" and k == 1:
                    at = 8.94
                at = max(at, 0)
                assert at < SLOTS_AHEAD + TURN, (kind, k)
                timed.append((at, kind, k))
        timed.sort(key=lambda step: (step[0] - SLOTS_AHEAD) % TURN)
        steps = [(kind, k, 1 if at < SLOTS_AHEAD else 0) for at, kind, k in timed]
        head_only = [
            (2.14, ("unit_genes", 0, 1)), (1.88, ("unit_high", 0, 1)), (1.35, ("unit_low", 0, 1)),
            (3.54, ("unit_genes", 1, 1)), (3.28, ("unit_high", 1, 1)), (2.75, ("unit_low", 1, 1)),
            (4.94, ("unit_genes", 2, 1)), (4.68, ("unit_high", 2, 1)), (4.15, ("unit_low", 2, 1)),
            (1.21, ("expert_weights", 0, 1)), (2.48, ("expert_gates", 0, 1)),
            (2.68, ("gates_turn", 0, 1)), (3.83, ("gates_keep", 0, 1)), (0.67, ("gates_store", 0, 1)),
        ]
        head = [step for at, step in sorted(
            [(at, (kind, k, 1)) for at, kind, k in timed if at < SLOTS_AHEAD] + head_only,
            key=lambda step: step[0])]
        last_turn = [step for step in steps if step[2] == 0]

        TB_KINDS = {"mix_turn": GROUPS, "plain": SEQS, "fit": SEQS, "attend": SEQS, "add_attended": SEQS, "finish": 1}

        def use_before(todo, i):
            ahead = todo[i][2]
            for kind, k, other in todo[i - 1::-1] if i else ():
                if kind in TB_KINDS:
                    return kind, k + (other - ahead) * TB_KINDS[kind]
            if todo is head:
                return None
            kind, k, other = [step for step in steps if step[0] in TB_KINDS][-1]
            return kind, k + (other - 1 - ahead) * TB_KINDS[kind]

        x_in = [sem(f"x_in{i}") for i in range(CHUNKS)]
        proj_in, consts_in, wo_in = sem("proj_in"), sem("consts_in"), sem("wo_in")
        up_ld = [sem(f"up_ld{i}") for i in range(2)]
        piece_high, piece_low = sem("piece_high"), sem("piece_low")
        made = sem("made")
        filled = sem("filled")
        v_step = sem("v_step")
        var_ready, std_ready = sem("var_ready"), sem("std_ready")
        rstd_ready, xn_even, xn_odd = sem("rstd_ready"), sem("xn_even"), sem("xn_odd")
        xT_turned, xT_kept, x_hi_kept, x_lo_kept = (sem(n) for n in ("xT_turned", "xT_kept", "x_hi_kept", "x_lo_kept"))
        projected, genes_kept, valued, values_kept = (sem(n) for n in (
            "projected", "genes_kept", "valued", "values_kept"))
        norm2_ready, norm_ready, clamped, logged = (sem(n) for n in (
            "norm2_ready", "norm_ready", "clamped", "logged"))
        unit_ready, g_hi_ready = sem("unit_ready"), sem("g_hi_ready")
        shifted, prob_ready, chosen_ready, counted, gates_ready = (sem(n) for n in (
            "shifted", "prob_ready", "chosen_ready", "counted", "gates_ready"))
        fourth_ready, kept_ready, inverted = sem("fourth_ready"), sem("kept_ready"), sem("inverted")
        weighed = sem("weighed")
        half_ready, genes_ready = sem("half_ready"), sem("genes_ready")
        gates_turned, gates_kept, logs_turned, logs_kept = (sem(n) for n in (
            "gates_turned", "gates_kept", "logs_turned", "logs_kept"))
        gates_stored, logs_stored = sem("gates_stored"), sem("logs_stored")
        gate_ld = [sem(f"gate_ld{i}") for i in range(G_RING)]
        log_ld = [sem(f"log_ld{i}") for i in range(L_RING)]
        zeroed = sem("zeroed")
        stored, let_on = sem("stored"), sem("let_on")

        built = Count("built", SEQS)
        pair_turned, pair_kept = Count("pair_turned", GROUPS), Count("pair_kept", GROUPS)
        scored, damped = Count("scored", CHUNK_HEADS), Count("damped", CHUNK_HEADS)
        windowed, correlated = Count("windowed", CHUNK_HEADS), Count("correlated", CHUNK_HEADS)
        squared2 = Count("squared2", CHUNK_HEADS)
        mix_done, mix_kept = Count("mix_done", GROUPS), Count("mix_kept", GROUPS)
        tb_written = {kind: Count(f"{kind}_written", n) for kind, n in TB_KINDS.items()}
        tb_read = {kind: Count(f"{kind}_read", n) for kind, n in TB_KINDS.items()}
        fitted, attended_ready = Count("fitted", SEQS), Count("attended_ready", SEQS)
        NORM_STEPS = 8
        norm_step = Count("norm_step", NORM_STEPS * SEQS)
        up1_done, up3_done = Count("up1_done", PAIRS), Count("up3_done", PAIRS)
        silu_done, glu_done = Count("silu_done", PAIRS), Count("glu_done", PAIRS)
        gated_done, down_done = Count("gated_done", PAIRS - 1), Count("down_done", PAIRS)
        biased = Count("biased", 1)
        high_done, low_done = Count("high_done", PAIRS), Count("low_done", PAIRS)
        y_kept, summed = Count("y_kept", 1), Count("summed", 1)

        def last_use(k, slot_of):
            return next(j for j in range(k - 1, k - 1 - len(slot_of), -1) if slot_of[j % len(slot_of)] == slot_of[k])

        block = ctx.enter_context(nc.Block())

        @block.sync
        def _(sp):
            for c in range(CHUNKS):
                q = slice(c * CHUNK_TILES, (c + 1) * CHUNK_TILES)
                sp.dma_start(x[:, q, :], tokens_in[:, q, :]).then_inc(x_in[c], 16)
            sp.dma_start(proj_w[:, :], project_in).then_inc(proj_in, 16)
            sp.dma_start(proj_b[:, :], bias_in.partition_broadcast(P)).then_inc(consts_in, 16)
            sp.dma_start(wo_b[:, :], out_bias_in.partition_broadcast(P)).then_inc(consts_in, 16)
            for i, (_, _, source) in enumerate(pieces):
                if i >= 2:
                    sp.wait_ge(piece_low, i - 1)
                sp.dma_start(up_stage[:, i % 2, 0:source.shape[1]], source).then_inc(up_ld[i % 2], 16)
            sp.dma_start(wo[:, :], attn_out_in).then_inc(wo_in, 16)

            sp.wait_ge(logs_kept, 1)
            for i in range(2):
                rows = logs_dram.rearrange("t h p -> (t h) p")[i * P:(i + 1) * P, :]
                sp.dma_start(rows, turned_log[:, i * P:(i + 1) * P]).then_inc(logs_stored, 16)
            sp.wait_ge(logs_stored, 32)

            def run(turn, todo):
                for i, (kind, k, ahead) in enumerate(todo):
                    c = turn + ahead if ahead else turn
                    if kind == "log_rows":
                        g = k
                        s, q = g // GPS, g % GPS
                        sp.wait_ge(damped.sem, damped.after(c, QUAD * (g - L_RING) + QUAD - 1))
                        src = logs_dram[bass.ds(c * CHUNK_TILES + s * SEQ_TILES, SEQ_TILES),
                                        q * QUAD:(q + 1) * QUAD, :]
                        sp.dma_start(row_log[g % L_RING][:, :, :, :],
                                     src.partition_broadcast(P)).then_inc(log_ld[g % L_RING], 16)
                    if kind == "gates_store":
                        sp.wait_ge(gates_kept, 1)
                        by_quarter = gates_dram.rearrange("e (c b p) -> b e c p", b=4, p=P)
                        for b in range(4):
                            sp.dma_start(by_quarter[b], turned[b * EXPERTS:(b + 1) * EXPERTS, :].rearrange(
                                "e (c p) -> e c p", p=P)).then_inc(gates_stored, 16)
                        sp.wait_ge(gates_stored, 16 * 4)
                        sp.wait_ge(piece_low, len(pieces))
                    if kind == "gate_rows" and k >= 1:
                        slot = (k - 1) % G_RING
                        sp.wait_ge(gated_done.sem, gated_done.after(c, k - 1 - G_RING))
                        for half in range(2):
                            row = gates_dram[2 * (k - 1) + half, bass.ds(c * CHUNK, CHUNK)]
                            sp.dma_start(gate_row[slot][half * 64:(half + 1) * 64, :],
                                         row.partition_broadcast(64)).then_inc(gate_ld[slot], 16)
                    if kind == "store":
                        sp.wait_ge(summed.sem, summed.after(c, 0))
                        sp.dma_start(tokens_out[:, bass.ds(c * CHUNK_TILES, CHUNK_TILES), :],
                                     x[:, bass.ds(c * CHUNK_TILES, CHUNK_TILES), :]).then_inc(stored, 16)

            run(-1, head)
            with sp.Fori(0, CHUNKS - 1) as turn:
                run(turn, steps)
            run(CHUNKS - 1, last_turn)
            sp.wait_ge(stored, 16 * CHUNKS)

        @block.gpsimd
        def _(pool):
            n = [0]

            def chain(ins):
                n[0] += 1
                ins.then_inc(filled, 1)
                pool.wait_ge(filled, n[0])

            chain(nc.gpsimd.memset(ident[:, :], 0.0))
            nc.gpsimd.affine_select(out=ident[:, :], in_=ident[:, :], compare_op=ALU.not_equal, fill=1.0, base=0,
                                    pattern=[[-1, P]], channel_multiplier=1).then_inc(made, 1)
            chain(nc.gpsimd.memset(ones[:, :], 1.0))
            nc.gpsimd.affine_select(out=causal[:, :], in_=ones[:, :], compare_op=ALU.is_ge, fill=0.0, base=0,
                                    pattern=[[1, P]], channel_multiplier=-1).then_inc(made, 1)
            nc.gpsimd.affine_select(out=behind[:, :], in_=ones[:, :], compare_op=ALU.is_ge, fill=0.0, base=0,
                                    pattern=[[-1, P]], channel_multiplier=1).then_inc(made, 1)
            nc.gpsimd.memset(ones_b[:, :], 1.0).then_inc(made, 1)
            chain(nc.gpsimd.memset(later_b[:, :], 0.0))
            nc.gpsimd.affine_select(out=later_b[:, :], in_=later_b[:, :], compare_op=ALU.is_ge, fill=-1.0, base=0,
                                    pattern=[[1, P]], channel_multiplier=-1).then_inc(made, 1)
            nc.gpsimd.memset(fresh_row, 1.0).then_inc(filled, 1)
            nc.gpsimd.memset(fresh_expert, 1.0).then_inc(filled, 1)
            n[0] += 2
            pool.wait_ge(filled, n[0])
            nc.gpsimd.memset(fresh_row[:, :, 0:1], 0.0).then_inc(made, 1)
            nc.gpsimd.memset(fresh_expert[:, :, 0:1], 0.0).then_inc(made, 1)
            nc.gpsimd.memset(pairs_tm[:, :, :, :, :], 0.0).then_inc(filled, 1)
            n[0] += 1
            for s in range(SEQS):
                nc.gpsimd.memset(v32[s][:, :, :, :], 0.0).then_inc(filled, 1)
                n[0] += 1
            pool.wait_ge(filled, n[0])
            for s in range(SEQS):
                ins = nc.gpsimd.memset(v32[s][:, :, :, HD:HD + 1], 1.0)
                n[0] += 1
                ins.then_inc(filled, 1)
            pool.wait_ge(rstd_ready, 1)
            for t in range(1, TILES, 2):
                nc.gpsimd.tensor_scalar(xn[:, t, :], x[:, t, :], moments[:, t, 0:1], rstd[:, t:t + 1],
                                        ALU.subtract, ALU.mult).then_inc(xn_odd, 1)
            def piece_rest(i):
                high, low, _ = pieces[i]
                pool.wait_ge(piece_high, i + 1)
                nc.gpsimd.tensor_tensor(low, up_stage[:, i % 2, 0:low.shape[1]], high.bitcast(f32),
                                        ALU.subtract).then_inc(piece_low, 1)

            def unit_low(q):
                r = slice(q * CHUNK_TILES, (q + 1) * CHUNK_TILES)
                pool.wait_ge(g_hi_ready, q + 1)
                nc.gpsimd.tensor_tensor(g_lo[:, r, :], unit[:, r, :], g_hi[:, r, :].bitcast(f32),
                                        ALU.subtract).then_inc(genes_ready, 1)

            for q in range(CHUNKS):
                cols = slice(q * CHUNK, (q + 1) * CHUNK)
                pool.wait_ge(x_hi_kept, q + 1)
                nc.gpsimd.tensor_tensor(x_lo[:, cols], xT[:, cols], x_hi[:, cols].bitcast(f32),
                                        ALU.subtract).then_inc(x_lo_kept, 1)
                piece_rest(q)
            piece_rest(CHUNKS)
            unit_low(0)
            for i in range(CHUNKS + 1, len(pieces)):
                piece_rest(i)

            pool.wait_ge(filled, n[0])
            pool.sem_inc(zeroed, 1)
            for count in (windowed, gated_done, biased):
                pool.sem_inc(count.sem, count.per)
            pool.wait_ge(consts_in, 32)
            pool.wait_ge(xn_even, TILES // 2)
            pool.wait_ge(xn_odd, TILES // 2)
            outside = pool.to_reg(-1.0)

            def go():
                pool.sem_inc(let_on, 1)

            def run(turn, todo):
                for i, (kind, k, ahead) in enumerate(todo):
                    c = turn + ahead if ahead else turn
                    if kind == "unit_low":
                        unit_low(k + 1)
                    if kind == "bias":
                        r = bass.ds(c * CHUNK_TILES, CHUNK_TILES)
                        nc.gpsimd.tensor_tensor(x[:, r, :], x[:, r, :],
                                                wo_b[:, :].unsqueeze(1).to_broadcast([P, CHUNK_TILES, D]),
                                                ALU.add).then_inc(biased.sem, 1)
                    if kind == "window":
                        pool.wait_ge(damped.sem, damped.after(c, k))
                        go()
                        t = damp[k % T_RING]
                        nc.gpsimd.affine_select(out=t[:, 0:3:2, :], in_=t[:, 0:3:2, :], compare_op=ALU.is_ge,
                                                fill=outside, base=0, pattern=[[0, 2], [1, P]], channel_multiplier=-1)
                        nc.gpsimd.affine_select(out=t[:, 1, :], in_=t[:, 1, :], compare_op=ALU.is_ge,
                                                fill=outside, base=0, pattern=[[-1, P]],
                                                channel_multiplier=1).then_inc(windowed.sem, 1)
                    if kind == "gate" and k >= 1:
                        slot = (k - 1) % G_RING
                        uses = (PAIRS - 1) // G_RING
                        pool.wait_ge(glu_done.sem, glu_done.after(c, k))
                        pool.wait_ge(gate_ld[slot], c * (32 * uses) + 32 * ((k - 1) // G_RING + 1))
                        nc.gpsimd.tensor_tensor(hidden[hidden_slot[k]], hidden[hidden_slot[k]],
                                                gate_row[slot][:, :], ALU.mult).then_inc(gated_done.sem, 1)

            run(-1, head)
            with pool.Fori(0, CHUNKS - 1) as turn:
                run(turn, steps)
            run(CHUNKS - 1, last_turn)

        @block.scalar
        def _(act):
            act.wait_ge(var_ready, 1)
            nc.scalar.activation(std[:, :], var_eps[:, :], ACT.Sqrt).then_inc(std_ready, 1)
            def keep_values(q):
                act.wait_ge(valued, q + 1)
                nc.scalar.activation(values[:, q * CHUNK_TILES:(q + 1) * CHUNK_TILES, :].rearrange("p t d -> p (t d)"),
                                     (Y, U)[q % 2][:, :], ACT.Copy).then_inc(values_kept, 1)

            def split(i):
                high = pieces[i][0]
                act.wait_ge(up_ld[i % 2], 16 * (i // 2 + 1))
                nc.scalar.activation(high, up_stage[:, i % 2, 0:high.shape[1]], ACT.Copy).then_inc(piece_high, 1)

            def unit_high(q):
                r = slice(q * CHUNK_TILES, (q + 1) * CHUNK_TILES)
                act.wait_ge(unit_ready, q + 1)
                nc.scalar.activation(g_hi[:, r, :], unit[:, r, :], ACT.Copy).then_inc(g_hi_ready, 1)

            for q in range(CHUNKS):
                cols = slice(q * CHUNK, (q + 1) * CHUNK)
                act.wait_ge(xT_turned, q + 1)
                nc.scalar.activation(xT[:, cols], S[q % 2][:, :], ACT.Copy).then_inc(xT_kept, 1)
                nc.scalar.activation(x_hi[:, cols], S[q % 2][:, :], ACT.Copy).then_inc(x_hi_kept, 1)
                if q >= 1:
                    keep_values(q - 1)
                    split(q - 1)
            keep_values(CHUNKS - 1)
            act.wait_ge(norm2_ready, CHUNKS)
            nc.scalar.activation(norm[:, :, :], norm2[:, :, :], ACT.Sqrt).then_inc(norm_ready, 1)
            split(CHUNKS - 1)
            act.wait_ge(shifted, 1)
            nc.scalar.activation(prob, shifted_logits, ACT.Exp).then_inc(prob_ready, 1)
            act.wait_ge(clamped, 1)
            nc.scalar.activation(norm[:, :, :], norm[:, :, :], ACT.Ln, scale=CORR_EPS ** -0.5).then_inc(logged, 1)
            act.wait_ge(logged, 1)
            nc.scalar.activation(half_log[:, :, :], norm[:, :, :], ACT.Copy, scale=0.5).then_inc(half_ready, 1)
            split(CHUNKS)
            act.wait_ge(logs_turned, 1)
            nc.scalar.activation(turned_log[:, :], TB[:, 0:2 * P], ACT.Copy).then_inc(logs_kept, 1)
            unit_high(0)
            for i in range(CHUNKS + 1, len(pieces)):
                split(i)

            for count in (damped, squared2, silu_done, high_done, y_kept):
                act.sem_inc(count.sem, count.per)

            def run(turn, todo):
                for i, (kind, k, ahead) in enumerate(todo):
                    c = turn + ahead if ahead else turn
                    if kind == "damp":
                        g, h = k // QUAD, k % QUAD
                        s = g // GPS
                        if h == 0:
                            act.wait_ge(log_ld[g % L_RING], c * (16 * GROUPS // L_RING) + 16 * (g // L_RING + 1))
                            act.wait_ge(built.sem, built.after(c, s))
                        act.wait_ge(correlated.sem, correlated.after(c, k - T_RING))
                        at = (g % GPS) * QUAD + h
                        rows = row_log[g % L_RING]
                        nc.scalar.activation(damp[k % T_RING][:, 0:2, :], rows[:, :, h, :], ACT.Tanh,
                                             bias=key_log[s][:, 0, at:at + 1])
                        nc.scalar.activation(damp[k % T_RING][:, 2, :], rows[:, 1, h, :], ACT.Tanh,
                                             bias=key_log[s][:, 1, at:at + 1]).then_inc(damped.sem, 1)
                    if kind == "unit_high":
                        unit_high(k + 1)
                    if kind == "gates_keep":
                        act.wait_ge(gates_turned, 1)
                        nc.scalar.activation(turned[:, :], Y[:, :], ACT.Copy).then_inc(gates_kept, 1)
                    if kind == "high":
                        if k == 0 and todo is head:
                            act.wait_ge(genes_ready, CHUNKS)
                        done = glu_done.after(c, 0) if k == 0 else gated_done.after(c, k - 1)
                        act.wait_ge((glu_done if k == 0 else gated_done).sem, done)
                        act.wait_ge(down_done.sem, down_done.after(c, last_use(k, hidden_slot)))
                        slot = hidden_slot[k]
                        nc.scalar.activation(hidden_hi[slot][:, :], hidden[slot][:, :],
                                             ACT.Copy).then_inc(high_done.sem, 1)
                    if kind == "square":
                        if k == QUAD and todo is head:
                            act.wait_ge(unit_ready, CHUNKS)
                        g, h = k // QUAD, k % QUAD
                        act.wait_ge(correlated.sem, correlated.after(c, k))
                        act.wait_ge(mix_done.sem, mix_done.after(c, g - 2))
                        nc.scalar.activation(corr2[g % 2][:, h, :], corr[g % 2][:, h, :], ACT.Square,
                                             scale=0.5).then_inc(squared2.sem, 1)
                    if kind == "plain_keep":
                        act.wait_ge(tb_written["plain"].sem, tb_written["plain"].after(c, k))
                        act.wait_ge(norm_step.sem, norm_step.after(c, NORM_STEPS * (k + 1) - 1 - NORM_STEPS * SEQS))
                        nc.scalar.activation(plain[k][:, :, :, :].rearrange("p a b c -> p (a b c)"),
                                             TB[:, 0:SEQ_TILES * HEADS * (HD + 1)],
                                             ACT.Copy).then_inc(tb_read["plain"].sem, 1)
                    if kind == "silu":
                        act.wait_ge(up1_done.sem, up1_done.after(c, k))
                        act.wait_ge(glu_done.sem, glu_done.after(c, k - 1))
                        nc.scalar.activation(silu, H1[:, :], ACT.Silu).then_inc(silu_done.sem, 1)
                    if kind == "attend_keep":
                        act.wait_ge(tb_written["attend"].sem, tb_written["attend"].after(c, k))
                        nc.scalar.activation(attended_T[:, :], TB[:, 0:SEQ], ACT.Copy).then_inc(tb_read["attend"].sem, 1)
                    if kind == "y_keep":
                        act.wait_ge(down_done.sem, down_done.after(c, PAIRS - 1))
                        act.wait_ge(tb_written["finish"].sem, tb_written["finish"].after(c, -1))
                        nc.scalar.activation(y_sb[:, :], Y[:, :], ACT.Copy).then_inc(y_kept.sem, 1)

            run(-1, head)
            act.wait_ge(genes_ready, CHUNKS)
            with act.Fori(0, CHUNKS - 1) as turn:
                run(turn, steps)
            run(CHUNKS - 1, last_turn)

        @block.vector
        def _(dve):
            n = [0]

            def chain(ins):
                n[0] += 1
                ins.then_inc(v_step, 1)
                dve.wait_ge(v_step, n[0])

            for q in range(CHUNKS):
                dve.wait_ge(x_in[q], 16)
                for t in range(q * CHUNK_TILES, (q + 1) * CHUNK_TILES):
                    last = nc.vector.bn_stats(stats[:, t, :], x[:, t, :])
            chain(last)
            for t in range(TILES):
                last = nc.vector.bn_aggr(moments[:, t, :], stats[:, t, :])
            chain(last)
            nc.vector.tensor_scalar(var_eps[:, :], moments[:, :, 1], LN_EPS, None, ALU.add).then_inc(var_ready, 1)
            dve.wait_ge(std_ready, 1)
            chain(nc.vector.reciprocal(rstd[:, :], std[:, :]))
            chain(nc.vector.tensor_tensor(newton[:, :], rstd[:, :], rstd[:, :], ALU.mult))
            dve.wait_ge(var_ready, 1)
            chain(nc.vector.tensor_tensor(newton[:, :], newton[:, :], var_eps[:, :], ALU.mult))
            chain(nc.vector.tensor_scalar(newton[:, :], newton[:, :], -0.5, 1.5, ALU.mult, ALU.add))
            nc.vector.tensor_tensor(rstd[:, :], rstd[:, :], newton[:, :], ALU.mult).then_inc(rstd_ready, 1)
            dve.wait_ge(rstd_ready, 1)
            for t in range(0, TILES, 2):
                nc.vector.tensor_scalar(xn[:, t, :], x[:, t, :], moments[:, t, 0:1], rstd[:, t:t + 1],
                                        ALU.subtract, ALU.mult).then_inc(xn_even, 1)
            dve.wait_ge(consts_in, 32)
            bias_b = proj_b[:, 0:D].unsqueeze(1).to_broadcast([P, 2, D])
            for q in range(CHUNKS):
                for i in range(q * CHUNK_TILES // 2, (q + 1) * CHUNK_TILES // 2):
                    dve.wait_ge(projected, i + 1)
                    both = (H1, H3)[i % 2][:, 0:2 * GL].rearrange("p (t w) -> p t w", w=GL)
                    nc.vector.tensor_copy(logits[:, 2 * i:2 * i + 2, :], both[:, :, D:GL])
                    last = nc.vector.tensor_tensor(genes[:, 2 * i:2 * i + 2, :], both[:, :, 0:D], bias_b, ALU.add)
                    last.then_inc(genes_kept, 1)
                dve.wait_ge(genes_kept, (q + 1) * CHUNK_TILES // 2)
                r = slice(q * CHUNK_TILES, (q + 1) * CHUNK_TILES)
                chain(nc.vector.tensor_tensor(squares[:, r, :], genes[:, r, :], genes[:, r, :], ALU.mult))
                nc.vector.tensor_reduce(norm2[:, r, :], squares[:, r, :].rearrange("p t (h d) -> p t h d", d=HD),
                                        AX.X, ALU.add).then_inc(norm2_ready, 1)

            for t in range(TILES):
                last = nc.vector.max(top8[:, t, :], logits[:, t, :])
            chain(last)
            chain(nc.vector.tensor_tensor(shifted_logits, logits[:, :, :],
                                          top8[:, :, 0:1].to_broadcast([P, TILES, EXPERTS]), ALU.subtract))
            nc.vector.tensor_tensor(per_tile[0][:, :], top8[:, :, TOP - 1], top8[:, :, 0],
                                    ALU.subtract).then_inc(fourth_ready, 1)
            nc.vector.tensor_scalar(shifted_logits, shifted_logits, -87.33, None, ALU.max).then_inc(shifted, 1)
            dve.wait_ge(fourth_ready, 1)
            chain(nc.vector.tensor_scalar(per_tile[0][:, :], per_tile[0][:, :], -87.33, None, ALU.max))
            dve.wait_ge(shifted, 1)
            dve.wait_ge(made, 7)
            fourth = per_tile[0][:, :].unsqueeze(2).to_broadcast([P, TILES, EXPERTS])
            chain(nc.vector.tensor_tensor(equal, shifted_logits, fourth, ALU.is_equal))
            nc.vector.tensor_tensor_scan(ranked.rearrange("p t e -> p (t e)"),
                                         fresh_row.rearrange("p t e -> p (t e)"),
                                         equal.rearrange("p t e -> p (t e)"), 0.0, ALU.mult, ALU.add)
            chain(nc.vector.tensor_tensor(above, shifted_logits, fourth, ALU.is_gt))
            chain(nc.vector.tensor_reduce(per_tile[1][:, :], above, AX.X, ALU.add))
            chain(nc.vector.tensor_scalar(per_tile[1][:, :], per_tile[1][:, :], -1.0, float(TOP), ALU.mult, ALU.add))
            left_b = per_tile[1][:, :].unsqueeze(2).to_broadcast([P, TILES, EXPERTS])
            chain(nc.vector.tensor_tensor(ranked, ranked, left_b, ALU.is_le))
            chain(nc.vector.tensor_tensor(equal, equal, ranked, ALU.mult))
            nc.vector.tensor_tensor(chosen, equal, above, ALU.add).then_inc(chosen_ready, 1)

            dve.wait_ge(norm_ready, 1)
            chain(nc.vector.tensor_scalar(norm2[:, :, :], norm[:, :, :], 1e-22, None, ALU.add))
            nc.vector.tensor_scalar(norm[:, :, :], norm[:, :, :], 1e-22, 1e14, ALU.max, ALU.min).then_inc(clamped, 1)
            nc.vector.reciprocal(inv_norm[:, :, :], norm2[:, :, :]).then_inc(inverted, 1)

            inv_b = inv_norm[:, :, :].unsqueeze(3).to_broadcast([P, TILES, HEADS, HD])

            def unit_genes(q):
                r = slice(q * CHUNK_TILES, (q + 1) * CHUNK_TILES)
                chain(nc.vector.tensor_tensor(unit[:, r, :].rearrange("p t (h d) -> p t h d", d=HD),
                                              genes[:, r, :].rearrange("p t (h d) -> p t h d", d=HD),
                                              inv_b[:, r], ALU.mult))
                chain(nc.vector.tensor_scalar(g_lo[:, r, :], unit[:, r, :], 0.0, None, ALU.max))
                nc.vector.scalar_tensor_tensor(out=unit[:, r, :], in0=unit[:, r, :], scalar=0.0, in1=g_lo[:, r, :],
                                               op0=ALU.min, op1=ALU.add).then_inc(unit_ready, 1)

            def expert_weights():
                dve.wait_ge(prob_ready, 1)
                chain(nc.vector.tensor_reduce(per_tile[0][:, :], prob, AX.X, ALU.add))
                chain(nc.vector.reciprocal(per_tile[2][:, :], per_tile[0][:, :]))
                share_b = per_tile[2][:, :].unsqueeze(2).to_broadcast([P, TILES, EXPERTS])
                nc.vector.tensor_tensor(weight, prob, share_b, ALU.mult).then_inc(weighed, 1)

            def expert_gates():
                dve.wait_ge(counted, 1)
                chain(nc.vector.tensor_tensor_scan(carried.rearrange("p e t -> p (e t)"),
                                                   fresh_expert.rearrange("p e t -> p (e t)"),
                                                   Y[:, :], 0.0, ALU.mult, ALU.add))
                chain(nc.vector.tensor_tensor(place.rearrange("p e t -> p (e t)"),
                                              carried.rearrange("p e t -> p (e t)"), U[:, :], ALU.add))
                nc.vector.scalar_tensor_tensor(out=kept, in0=place, scalar=float(CAPACITY),
                                               in1=chosen.rearrange("p t e -> p e t"), op0=ALU.is_le,
                                               op1=ALU.mult).then_inc(kept_ready, 1)
                dve.wait_ge(kept_ready, 1)
                dve.wait_ge(weighed, 1)
                nc.vector.tensor_tensor(gates[:, :, :], weight, kept.rearrange("p e t -> p t e"),
                                        ALU.mult).then_inc(gates_ready, 1)

            dve.wait_ge(inverted, 1)
            unit_genes(0)

            for count in (built, pair_kept, mix_kept, correlated, glu_done, low_done, *tb_read.values(), fitted, attended_ready, norm_step, summed):
                dve.sem_inc(count.sem, count.per)
            dve.wait_ge(half_ready, 1)
            dve.wait_ge(values_kept, CHUNKS)
            dve.wait_ge(zeroed, 1)

            def run(turn, todo):
                for i, (kind, k, ahead) in enumerate(todo):
                    c = turn + ahead if ahead else turn
                    if kind == "unit_genes":
                        unit_genes(k + 1)
                    if kind == "expert_weights":
                        expert_weights()
                    if kind == "expert_gates":
                        expert_gates()
                    if kind == "low":
                        if k == 0 and todo is head:
                            dve.wait_ge(genes_ready, CHUNKS)
                        dve.wait_ge(high_done.sem, high_done.after(c, k))
                        dve.wait_ge(down_done.sem, down_done.after(c, last_use(k, hidden_slot)))
                        slot = hidden_slot[k]
                        nc.vector.tensor_tensor(hidden_lo[slot][:, :], hidden[slot][:, :],
                                                hidden_hi[slot][:, :].bitcast(f32),
                                                ALU.subtract).then_inc(low_done.sem, 1)
                    if kind == "build":
                        s = k
                        rows = bass.ds(c * CHUNK_TILES + s * SEQ_TILES, SEQ_TILES)
                        dve.wait_ge(genes_ready, c + 1)
                        dve.wait_ge(tb_written["plain"].sem, tb_written["plain"].after(c, k - SEQS))
                        dve.wait_ge(pair_turned.sem, pair_turned.after(c, s * GPS - 1))
                        dve.wait_ge(mix_done.sem, mix_done.after(c, (s + 1) * GPS - 1 - GROUPS))
                        dve.wait_ge(damped.sem, damped.after(c, (s + 1) * GPS * QUAD - 1 - CHUNK_HEADS))

                        def heads(buf):
                            return buf.rearrange("p t (h d) -> p (t h) d", d=HD)

                        def part(which, at):
                            return pairs_tm[:, which].rearrange("p t h w -> p (t h) w")[:, :, at * HD:(at + 1) * HD]

                        def twice(which, step):
                            both = pairs_tm[:, which].rearrange("p t h (j d) -> p (t h) j d", d=HD)
                            return both[:, :, 0:step + 1:step, :]

                        hi, lo = heads(g_hi[:, rows, :].bitcast(f32)), heads(g_lo[:, rows, :])
                        hi2 = hi.unsqueeze(2).to_broadcast([P, SEQ_TILES * HEADS, 2, HD])
                        for dst, src in ((twice(0, 2), hi2), (part(0, 1), lo), (twice(1, 1), hi2), (part(1, 2), lo)):
                            nc.vector.tensor_copy(dst, src)
                        bias = proj_b[:, D:2 * D].rearrange("p (h d) -> p h d", d=HD)
                        nc.vector.tensor_tensor(v32[s][:, :, :, 0:HD],
                                                values[:, rows, :].rearrange("p t (h d) -> p t h d", d=HD),
                                                bias.unsqueeze(1).to_broadcast([P, SEQ_TILES, HEADS, HD]), ALU.add)
                        nc.vector.tensor_copy(key_log[s][:, :, :], half_log[:, rows, :]).then_inc(built.sem, 1)
                    if kind == "correlate":
                        g, h = k // QUAD, k % QUAD
                        dve.wait_ge(scored.sem, scored.after(c, k))
                        dve.wait_ge(windowed.sem, windowed.after(c, k))
                        dve.wait_ge(mix_done.sem, mix_done.after(c, g - 2))
                        nc.vector.scalar_tensor_tensor(
                            out=corr[g % 2][:, h, :], in0=damp[k % T_RING][:, :, :].rearrange("p a b -> p (a b)"),
                            scalar=1.0, in1=S[k % 2][:, 0:BANDS * P], op0=ALU.add,
                            op1=ALU.mult).then_inc(correlated.sem, 1)
                    if kind == "pair_keep":
                        dve.wait_ge(pair_turned.sem, pair_turned.after(c, k))
                        dve.wait_ge(scored.sem, scored.after(c, QUAD * (k - 2) + QUAD - 1))
                        nc.vector.tensor_copy(pairs_T[k % 2][:, :, :],
                                              TA[:, :].rearrange("p (w q) -> p w q", w=2)).then_inc(pair_kept.sem, 1)
                    if kind == "mix_keep":
                        dve.wait_ge(mix_done.sem, mix_done.after(c, k))
                        if k == 0 and todo is head:
                            dve.wait_ge(piece_low, len(pieces))
                        dve.wait_ge(tb_written["mix_turn"].sem, tb_written["mix_turn"].after(c, k - 1))
                        nc.vector.tensor_copy(mixed.rearrange("p a b -> p (a b)"), U[:, :]).then_inc(mix_kept.sem, 1)
                    if kind == "sum_keep":
                        dve.wait_ge(tb_written["mix_turn"].sem, tb_written["mix_turn"].after(c, k))
                        s, q = k // GPS, k % GPS
                        src = TB[:, :].rearrange("p (a h w) -> p a h w", h=QUAD, w=SLOTS)[:, :, :, 0:HD + 1]
                        dst = sums[s][:, :, :, q * QUAD:(q + 1) * QUAD, :].rearrange("p a b h w -> p (a b) h w")
                        nc.vector.tensor_copy(dst, src).then_inc(tb_read["mix_turn"].sem, 1)
                    if kind == "glu":
                        dve.wait_ge(up3_done.sem, up3_done.after(c, k))
                        dve.wait_ge(silu_done.sem, silu_done.after(c, k))
                        dve.wait_ge(low_done.sem, low_done.after(c, last_use(k, hidden_slot)))
                        nc.vector.tensor_tensor(hidden[hidden_slot[k]], silu, H3[:, :],
                                                ALU.mult).then_inc(glu_done.sem, 1)
                    first = NORM_STEPS * k

                    def own(j):
                        dve.wait_ge(norm_step.sem, norm_step.after(c, first + j))

                    if kind == "denominator":
                        dve.wait_ge(tb_read["mix_turn"].sem, tb_read["mix_turn"].after(c, (k + 1) * GPS - 1))
                        nc.vector.tensor_scalar(mean_d[:, :, :], sums[k][:, 0, :, :, HD], 1.0 / (4 * SEQ), 1.0,
                                                ALU.mult, ALU.add).then_inc(norm_step.sem, 1)
                        own(0)
                        nc.vector.reciprocal(inv[:, :, :], mean_d[:, :, :]).then_inc(fitted.sem, 1)
                    if kind == "weigh":
                        dve.wait_ge(tb_written["fit"].sem, tb_written["fit"].after(c, k))
                        nc.vector.reciprocal(total[:, :], TB[:, 0:HEADS]).then_inc(tb_read["fit"].sem, 1)
                        dve.wait_ge(tb_read["fit"].sem, tb_read["fit"].after(c, k))
                        dve.wait_ge(fitted.sem, fitted.after(c, k))
                        nc.vector.scalar_tensor_tensor(
                            out=alpha[:, :, :], in0=inv[:, :, :], scalar=0.25,
                            in1=total[:, :].unsqueeze(1).to_broadcast([P, SEQ_TILES, HEADS]),
                            op0=ALU.mult, op1=ALU.mult).then_inc(norm_step.sem, 1)
                        own(1)
                        M = SEQ_TILES * HEADS
                        a_b = alpha[:, :, :].rearrange("p t h -> p (t h)").unsqueeze(2).to_broadcast([P, M, HD + 1])

                        def rows(buf):
                            return buf.rearrange("p t h w -> p (t h) w")

                        first_sum, second_sum = rows(sums[k][:, 0]), rows(sums[k][:, 1])
                        nc.vector.scalar_tensor_tensor(out=rows(num[:, :, :, :]), in0=second_sum, scalar=2.0, in1=a_b,
                                                       op0=ALU.mult, op1=ALU.mult).then_inc(norm_step.sem, 1)
                        own(2)
                        nc.vector.tensor_tensor(rows(num2[:, :, :, :]), rows(num[:, :, :, :]), first_sum,
                                                ALU.add).then_inc(norm_step.sem, 1)
                        own(3)
                        nc.vector.tensor_tensor(rows(num[:, :, :, :]), rows(num2[:, :, :, :]), a_b,
                                                ALU.mult).then_inc(norm_step.sem, 1)
                        own(4)
                        dve.wait_ge(tb_read["plain"].sem, tb_read["plain"].after(c, k))
                        nc.vector.tensor_tensor(rows(num2[:, :, :, :]), rows(num[:, :, :, :]), rows(plain[k][:, :, :, :]),
                                                ALU.add).then_inc(norm_step.sem, 1)
                        own(5)
                        nc.vector.reciprocal(inv_sum[:, :, :], num2[:, :, :, HD]).then_inc(norm_step.sem, 1)
                        own(6)
                        dve.wait_ge(tb_written["attend"].sem, tb_written["attend"].after(c, k - 1))
                        nc.vector.tensor_tensor(
                            attended[:, :, :].rearrange("p t (h w) -> p (t h) w", w=HD),
                            rows(num2[:, :, :, 0:HD]),
                            inv_sum[:, :, :].rearrange("p t h -> p (t h)").unsqueeze(2).to_broadcast([P, M, HD]),
                            ALU.mult).then_inc(attended_ready.sem, 1)
                        dve.wait_ge(attended_ready.sem, attended_ready.after(c, k))
                        dve.sem_inc(norm_step.sem, 1)
                    if kind == "add_keep":
                        dve.wait_ge(tb_written["add_attended"].sem, tb_written["add_attended"].after(c, k))
                        dve.wait_ge(biased.sem, biased.after(c, 0))
                        r = bass.ds(c * CHUNK_TILES + k * SEQ_TILES, SEQ_TILES)
                        nc.vector.tensor_tensor(x[:, r, :], TB[:, 0:SEQ_TILES * D].rearrange("p (t d) -> p t d", d=D),
                                                x[:, r, :], ALU.add).then_inc(tb_read["add_attended"].sem, 1)
                    if kind == "finish_keep":
                        dve.wait_ge(tb_written["finish"].sem, tb_written["finish"].after(c, 0))
                        dve.wait_ge(tb_read["add_attended"].sem, tb_read["add_attended"].after(c, SEQS - 1))
                        r = bass.ds(c * CHUNK_TILES, CHUNK_TILES)
                        nc.vector.tensor_tensor(x[:, r, :], TB[:, :].rearrange("p (t d) -> p t d", d=D),
                                                x[:, r, :], ALU.add).then_inc(summed.sem, 1)
                        dve.wait_ge(summed.sem, summed.after(c, 0))
                        dve.sem_inc(tb_read["finish"].sem, 1)

            run(-1, head)
            dve.wait_ge(genes_ready, CHUNKS)
            dve.wait_ge(piece_low, len(pieces))
            with dve.Fori(0, CHUNKS - 1) as turn:
                run(turn, steps)
            run(CHUNKS - 1, last_turn)

        @block.tensor
        def _(pe):
            pe.wait_ge(made, 7)
            pe.wait_ge(proj_in, 16)

            def turn_tokens(q):
                if q >= 2:
                    pe.wait_ge(x_hi_kept, q - 1)
                pe.wait_ge(xn_even, (q + 1) * CHUNK_TILES // 2)
                pe.wait_ge(xn_odd, (q + 1) * CHUNK_TILES // 2)
                for j in range(CHUNK_TILES):
                    last = nc.tensor.transpose(S[q % 2][:, j * P:(j + 1) * P], xn[:, q * CHUNK_TILES + j, :],
                                               ident[:, :])
                last.then_inc(xT_turned, 1)

            turn_tokens(0)
            for q in range(CHUNKS):
                if q + 1 < CHUNKS:
                    turn_tokens(q + 1)
                pe.wait_ge(xT_kept, q + 1)
                for i in range(q * CHUNK_TILES // 2, (q + 1) * CHUNK_TILES // 2):
                    if i >= 2:
                        pe.wait_ge(genes_kept, i - 1)
                    for j in range(2):
                        t = 2 * i + j
                        last = nc.tensor.matmul((H1, H3)[i % 2][:, j * GL:(j + 1) * GL], xT[:, t * P:(t + 1) * P],
                                                proj_w[:, 0:GL], start=True, stop=True, skip_group_check=True)
                    last.then_inc(projected, 1)
                if q >= 2:
                    pe.wait_ge(values_kept, q - 1)
                for j in range(CHUNK_TILES):
                    t = q * CHUNK_TILES + j
                    last = nc.tensor.matmul((Y, U)[q % 2][:, j * P:(j + 1) * P], xT[:, t * P:(t + 1) * P],
                                            proj_w[:, GL:PROJ], start=True, stop=True, skip_group_check=True)
                last.then_inc(valued, 1)
            pe.wait_ge(chosen_ready, 1)
            pe.wait_ge(values_kept, CHUNKS)
            flat = chosen.rearrange("p t e -> p e t")
            nc.tensor.matmul(U[:, :], later_b[:, :], flat, start=True, stop=True)
            nc.tensor.matmul(Y[:, :], ones_b[:, :], flat, start=True, stop=True).then_inc(counted, 1)
            pe.wait_ge(half_ready, 1)
            for i in range(2):
                last = nc.tensor.transpose(TB[:, i * P:(i + 1) * P],
                                           half_log[:, 8 * i:8 * (i + 1), :].rearrange("p t h -> p (t h)"),
                                           ident[:, :])
            last.then_inc(logs_turned, 1)
            pe.wait_ge(logs_kept, 1)
            pe.wait_ge(x_hi_kept, CHUNKS)
            pe.wait_ge(piece_low, 4)
            pe.wait_ge(x_lo_kept, CHUNKS)
            pe.wait_ge(wo_in, 16)

            for count in (pair_turned, scored, mix_done, *tb_written.values(), up1_done, up3_done, down_done):
                pe.sem_inc(count.sem, count.per)

            def run(turn, todo):
                for i, (kind, k, ahead) in enumerate(todo):
                    c = turn + ahead if ahead else turn

                    def take_tb():
                        before = use_before(todo, i)
                        if before:
                            read = tb_read[before[0]]
                            pe.wait_ge(read.sem, read.after(c, before[1]))

                    if kind == "gates_turn":
                        pe.wait_ge(gates_ready, 1)
                        for i in range(4):
                            last = nc.tensor.transpose(Y[:, i * P:(i + 1) * P],
                                                       gates[:, 4 * i:4 * (i + 1), :].rearrange("p t e -> p (t e)"),
                                                       ident[:, :])
                        last.then_inc(gates_turned, 1)
                    if kind == "pair_turn":
                        s, q = k // GPS, k % GPS
                        pe.wait_ge(built.sem, built.after(c, s))
                        pe.wait_ge(pair_kept.sem, pair_kept.after(c, k - 1))
                        for which in range(2):
                            for t in range(SEQ_TILES):
                                src = pairs_tm[:, which, t, q * QUAD:(q + 1) * QUAD, :]
                                at = which * SEQ + t * P
                                last = nc.tensor.transpose(TA[:, at:at + P], src.rearrange("p h w -> p (h w)"),
                                                           ident[:, :])
                        last.then_inc(pair_turned.sem, 1)
                    if kind == "score":
                        g, h = k // QUAD, k % QUAD
                        pe.wait_ge(pair_kept.sem, pair_kept.after(c, g))
                        pe.wait_ge(correlated.sem, correlated.after(c, k - 2))
                        rows = slice(h * SLOTS, h * SLOTS + TERMS)
                        keys, queries = pairs_T[g % 2][rows, 0, :], pairs_T[g % 2][rows, 1, :]
                        nc.tensor.matmul(S[k % 2][:, 0:SEQ], keys[:, 0:P], queries, start=True, stop=True)
                        nc.tensor.matmul(S[k % 2][:, SEQ:SEQ + P], keys[:, P:SEQ], queries[:, P:SEQ],
                                         start=True, stop=True).then_inc(scored.sem, 1)
                    if kind in ("mix_corr", "mix_square"):
                        s, q = k // GPS, k % GPS
                        pe.wait_ge(mix_kept.sem, mix_kept.after(c, k - 1))
                        if kind == "mix_corr" and k == 0 and todo is head:
                            pe.wait_ge(gates_ready, 1)
                        if kind == "mix_corr":
                            power, src, done = 0, corr[k % 2], None
                            pe.wait_ge(correlated.sem, correlated.after(c, QUAD * k + QUAD - 1))
                        else:
                            power, src, done = 1, corr2[k % 2], mix_done
                            pe.wait_ge(squared2.sem, squared2.after(c, QUAD * k + QUAD - 1))
                        for t in range(SEQ_TILES):
                            for h in range(QUAD):
                                cols = slice(power * SEQ + t * P, power * SEQ + SEQ)
                                rhs = src[:, h, 0:SEQ] if t == 0 else src[:, h, SEQ:SEQ + P]
                                last = nc.tensor.matmul(U[h * SLOTS:(h + 1) * SLOTS, cols],
                                                        v32[s][:, t, q * QUAD + h, :], rhs,
                                                        start=(t == 0), stop=(t == 1), skip_group_check=True)
                        if done:
                            last.then_inc(done.sem, 1)
                    if kind == "mix_turn":
                        pe.wait_ge(mix_kept.sem, mix_kept.after(c, k))
                        take_tb()
                        for power in range(2):
                            for t in range(SEQ_TILES):
                                at = (power * SEQ_TILES + t) * P
                                last = nc.tensor.transpose(TB[:, at:at + P], mixed[:, power, t * P:(t + 1) * P], ident[:, :])
                        last.then_inc(tb_written["mix_turn"].sem, 1)
                    if kind == "plain":
                        pe.wait_ge(built.sem, built.after(c, k))
                        take_tb()
                        W = HEADS * (HD + 1)
                        v9 = [v32[k][:, t, :, 0:HD + 1] for t in range(SEQ_TILES)]
                        nc.tensor.matmul(TB[:, 0:W], causal[:, :], v9[0], start=True, stop=True,
                                         skip_group_check=True)
                        nc.tensor.matmul(TB[:, W:2 * W], behind[:, :], v9[0], start=True, stop=False,
                                         skip_group_check=True)
                        nc.tensor.matmul(TB[:, W:2 * W], causal[:, :], v9[1], start=False, stop=True,
                                         skip_group_check=True).then_inc(tb_written["plain"].sem, 1)
                    if kind == "fit":
                        pe.wait_ge(fitted.sem, fitted.after(c, k))
                        take_tb()
                        nc.tensor.matmul(TB[:, 0:HEADS], ones[:, :], inv[:, 0, :], start=True, stop=False)
                        nc.tensor.matmul(TB[:, 0:HEADS], ones[:, :], inv[:, 1, :], start=False,
                                         stop=True).then_inc(tb_written["fit"].sem, 1)
                    if kind == "attend":
                        pe.wait_ge(attended_ready.sem, attended_ready.after(c, k))
                        take_tb()
                        for t in range(SEQ_TILES):
                            last = nc.tensor.transpose(TB[:, t * P:(t + 1) * P], attended[:, t, :], ident[:, :])
                        last.then_inc(tb_written["attend"].sem, 1)
                    if kind == "add_attended":
                        pe.wait_ge(tb_read["attend"].sem, tb_read["attend"].after(c, k))
                        take_tb()
                        for t in range(SEQ_TILES):
                            last = nc.tensor.matmul(TB[:, t * D:(t + 1) * D], attended_T[:, t * P:(t + 1) * P],
                                                    wo[:, :], start=True, stop=True, skip_group_check=True)
                        last.then_inc(tb_written["add_attended"].sem, 1)
                    if kind in ("up1", "up3"):
                        cols = bass.ds(c * CHUNK, CHUNK)
                        xs_hi, xs_lo = x_hi[:, cols], x_lo[:, cols]
                        if kind == "up1":
                            which, bank, done = 0, H1, up1_done
                            pe.wait_ge(silu_done.sem, silu_done.after(c, k - 1))
                        else:
                            which, bank, done = 1, H3, up3_done
                            pe.wait_ge(glu_done.sem, glu_done.after(c, k - 1))
                        nc.tensor.matmul(bank[:, :], up_hi[:, k, which, :], xs_hi, start=True, stop=False)
                        nc.tensor.matmul(bank[:, :], up_hi[:, k, which, :], xs_lo, start=False, stop=False)
                        nc.tensor.matmul(bank[:, :], up_lo[:, k, which, :], xs_hi, start=False,
                                         stop=True).then_inc(done.sem, 1)
                    if kind == "down":
                        slot = hidden_slot[k]
                        pe.wait_ge(low_done.sem, low_done.after(c, k))
                        if k == 0:
                            pe.wait_ge(y_kept.sem, y_kept.after(c, -1))
                        if k == 0 and todo is head:
                            pe.wait_ge(gates_kept, 1)
                            pe.wait_ge(piece_low, len(pieces))
                        nc.tensor.matmul(Y[:, :], down_hi[:, k, :], hidden_hi[slot][:, :], start=(k == 0), stop=False)
                        nc.tensor.matmul(Y[:, :], down_hi[:, k, :], hidden_lo[slot][:, :], start=False, stop=False)
                        nc.tensor.matmul(Y[:, :], down_lo[:, k, :], hidden_hi[slot][:, :], start=False,
                                         stop=(k == PAIRS - 1)).then_inc(down_done.sem, 1)
                    if kind == "finish":
                        pe.wait_ge(y_kept.sem, y_kept.after(c, 0))
                        take_tb()
                        for t in range(CHUNK_TILES):
                            last = nc.tensor.transpose(TB[:, t * P:(t + 1) * P], y_sb[:, t * P:(t + 1) * P],
                                                       ident[:, :])
                        last.then_inc(tb_written["finish"].sem, 1)

            run(-1, head)
            pe.wait_ge(gates_kept, 1)
            pe.wait_ge(piece_low, len(pieces))
            for kind, k, _ in head:
                if kind in TB_KINDS:
                    pe.wait_ge(tb_read[kind].sem, tb_read[kind].after(0, k))
            with pe.Fori(0, CHUNKS - 1) as turn:
                run(turn, steps)
            run(CHUNKS - 1, last_turn)


def kernel(L0_attn_x, L0_attn_Wg, L0_attn_bg, L0_attn_Wv, L0_attn_bv, L0_attn_Wo, L0_attn_bo, L0_ffn_Wg,
           L0_ffn_W1, L0_ffn_W2, L0_ffn_W3, L0_ffn_Ws1, L0_ffn_Ws2, L0_ffn_Ws3):
    import concourse.bacc as bacc
    from concourse.bass_utils import run_bass_kernel_spmd

    B, T, D = L0_attn_x.shape
    E, _, H = L0_ffn_W1.shape

    def tiles(a):
        return a.reshape(B * T // P, P, D).transpose(1, 0, 2)

    def up_pairs(shared, experts):
        return np.concatenate([shared[:, None, :], experts.transpose(1, 0, 2).reshape(D, E // 2, 2 * H)], axis=1)

    arrays = {
        "tokens_in": tiles(L0_attn_x),
        "project_in": np.concatenate([L0_attn_Wg.T, L0_ffn_Wg, L0_attn_Wv.T], axis=1),
        "bias_in": np.concatenate([L0_attn_bg, L0_attn_bv]),
        "out_bias_in": L0_attn_bo,
        "attn_out_in": L0_attn_Wo.T,
        "up_in": np.stack([up_pairs(L0_ffn_Ws1, L0_ffn_W1), up_pairs(L0_ffn_Ws3, L0_ffn_W3)], axis=2),
        "down_in": np.concatenate([L0_ffn_Ws2[:, None, :],
                                   L0_ffn_W2.reshape(E // 2, 2 * H, D).transpose(1, 0, 2)], axis=1),
    }
    arrays = {k: np.ascontiguousarray(a) for k, a in arrays.items()}
    nc = bacc.Bacc("TRN2", target_bir_lowering=False, num_devices=1)
    args = [nc.dram_tensor(k, a.shape, mybir.dt.from_np(a.dtype), kind="ExternalInput").ap()
            for k, a in arrays.items()]
    args.append(nc.dram_tensor("tokens_out", (P, B * T // P, D), mybir.dt.float32, kind="ExternalOutput").ap())
    windowed_attention_and_routed_experts(nc, *args)
    r = run_bass_kernel_spmd(nc, [arrays], core_ids=[0])
    return r.results[0]["tokens_out"].transpose(1, 0, 2).reshape(B, T, D)
```
